# Optimizing a Trainium2 kernel written in Bass

```python
import numpy as np
import jax
import jax.numpy as jnp

def _softmax(x, axis=-1):
    return jax.nn.softmax(x, axis=axis)

def _gelu(x):
    return jax.nn.gelu(x, approximate=True)

def _silu(x):
    return jax.nn.silu(x)

def _sigmoid(x):
    return jax.nn.sigmoid(x)

def _layernorm(x, axis=-1, eps=1e-05):
    m = jnp.mean(x, axis=axis, keepdims=True)
    v = jnp.var(x, axis=axis, keepdims=True)
    return (x - m) / jnp.sqrt(v + eps)

def _scatter_add(tgt, idx, src, axis=0):
    return tgt.at[idx].add(src)

def _segment_sum(src, seg, n):
    return jax.ops.segment_sum(src, seg, n)
kernel_name = 'mk_flamingo_gated_d1_seqx_r2_fe564e'

def setup_inputs(seed: int=0):
    np.random.seed(seed)
    _w = jnp.asarray

    def _rec_inputs():
        import jax
        import jax.numpy as jnp
        _rk = jax.random.key(seed)
        x = -0.0002928 + 1 * jax.random.normal(jax.random.fold_in(_rk, 1), (2, 2048, 512), jnp.float32)
        _lenS = 2048 - jax.random.randint(jax.random.fold_in(_rk, 7), (2,), 0, max(1, 2048 // 4) + 1, jnp.int32)
        _lenS2 = 77 - jax.random.randint(jax.random.fold_in(_rk, 8), (2,), 0, max(1, 77 // 4) + 1, jnp.int32)
        _ctx_1024P = jax.random.normal(jax.random.fold_in(_rk, 11), (2, 16, 512), jnp.float32)
        _ctx_1024c = jax.random.dirichlet(jax.random.fold_in(_rk, 511), 0.3 * jnp.ones((16,), jnp.float32), (2, 77))
        _ctx_1024t = jnp.einsum('bsk,bkd->bsd', _ctx_1024c, _ctx_1024P)
        _ctx_1024t = _ctx_1024t * jax.lax.rsqrt(jnp.mean(jnp.square(_ctx_1024t)) + 1e-12) * 0.953939
        ctx_1024 = 2.81802e-05 + 1.00001 * (_ctx_1024t + 0.3 * jax.random.normal(jax.random.fold_in(_rk, 611), (2, 77, 512), jnp.float32))
        _g = jax.random.normal(jax.random.fold_in(_rk, 9001), (2, 1), jnp.float32)
        _g = jnp.sign(_g) * jnp.maximum(jnp.abs(_g), 1.0) + (_g == 0) * 1.0
        g_xattn = _g[0]
        g_ffn = _g[1]
        return (x, ctx_1024, g_xattn, g_ffn)
    x, ctx_1024, g_xattn, g_ffn = _rec_inputs()

    def _L0_xattn_setup():
        import jax, jax.numpy as jnp
        import numpy as np
        D_MODEL = 512
        N_HEADS = 16
        HEAD_DIM = D_MODEL // N_HEADS
        key = jax.random.key(seed)
        k1, k2, k3, k4, k5, k6 = jax.random.split(key, 6)
        B, T_q, T_kv = (4, 512, 2048)
        s = 1.0 / np.sqrt(D_MODEL)
        return {'query': jax.random.normal(k1, (B, T_q, D_MODEL), dtype=jnp.float32), 'kv_source': jax.random.normal(k2, (B, T_kv, D_MODEL), dtype=jnp.float32), 'w_q': jax.random.normal(k3, (D_MODEL, D_MODEL), dtype=jnp.float32) * s, 'w_k': jax.random.normal(k4, (D_MODEL, D_MODEL), dtype=jnp.float32) * s, 'w_v': jax.random.normal(k5, (D_MODEL, D_MODEL), dtype=jnp.float32) * s, 'w_o': jax.random.normal(k6, (D_MODEL, D_MODEL), dtype=jnp.float32) * s}
    _L0_xattn_all = _L0_xattn_setup()
    _L0_xattn_in = {k: v for k, v in _L0_xattn_all.items() if k in ('w_q', 'w_k', 'w_v', 'w_o')}
    del _L0_xattn_all

    def _L0_ffn_setup():
        import jax, jax.numpy as jnp
        import numpy as np
        EPS = 1e-06
        LN_EPS = 1e-05

        def _absmean_core(W):
            gamma = jnp.mean(jnp.abs(W)) + EPS
            Ws = W / gamma
            Wq = jnp.sign(Ws) * jnp.minimum(jnp.round(jnp.abs(Ws)), 1.0)
            return (Wq, gamma)

        @jax.custom_vjp
        def absmean(W):
            return _absmean_core(W)[0]

        def _absmean_fwd(W):
            Wq, gamma = _absmean_core(W)
            return (Wq, gamma)

        def _absmean_bwd(gamma, g):
            return (g / gamma,)
        absmean.defvjp(_absmean_fwd, _absmean_bwd)

        def layernorm(x, w, b, eps=LN_EPS):
            mu = jnp.mean(x, axis=-1, keepdims=True)
            var = jnp.mean((x - mu) ** 2, axis=-1, keepdims=True)
            return (x - mu) * jax.lax.rsqrt(var + eps) * w + b
        key = jax.random.key(seed)
        k1, k2, k3 = jax.random.split(key, 3)
        d, h = (512, 2048)
        B, T = (8, 1024)
        return {'x': jax.random.normal(k1, (B, T, d), jnp.float32), 'W_fc': jax.random.normal(k2, (h, d), jnp.float32), 'ln_w': jnp.ones((h,), jnp.float32), 'ln_b': jnp.zeros((h,), jnp.float32), 'W_proj': jax.random.normal(k3, (d, h), jnp.float32)}
    _L0_ffn_all = _L0_ffn_setup()
    _L0_ffn_in = {k: v for k, v in _L0_ffn_all.items() if k in ('W_fc', 'ln_w', 'ln_b', 'W_proj')}
    del _L0_ffn_all
    return {'x': x, 'ctx_1024': ctx_1024, 'g_xattn': g_xattn, 'g_ffn': g_ffn, 'L0_xattn_w_q': _L0_xattn_in['w_q'], 'L0_xattn_w_k': _L0_xattn_in['w_k'], 'L0_xattn_w_v': _L0_xattn_in['w_v'], 'L0_xattn_w_o': _L0_xattn_in['w_o'], 'L0_ffn_W_fc': _L0_ffn_in['W_fc'], 'L0_ffn_ln_w': _L0_ffn_in['ln_w'], 'L0_ffn_ln_b': _L0_ffn_in['ln_b'], 'L0_ffn_W_proj': _L0_ffn_in['W_proj']}

def reference(x, ctx_1024, g_xattn, g_ffn, L0_xattn_w_q, L0_xattn_w_k, L0_xattn_w_v, L0_xattn_w_o, L0_ffn_W_fc, L0_ffn_ln_w, L0_ffn_ln_b, L0_ffn_W_proj):
    import jax
    import jax.numpy as jnp

    def _L0_xattn_ref(query, kv_source, w_q, w_k, w_v, w_o):
        import jax, jax.numpy as jnp
        import numpy as np
        D_MODEL = 512
        N_HEADS = 16
        HEAD_DIM = D_MODEL // N_HEADS
        B, T_q, _ = query.shape
        T_kv = kv_source.shape[1]
        q = (query @ w_q.T).reshape(B, T_q, N_HEADS, HEAD_DIM)
        k = (kv_source @ w_k.T).reshape(B, T_kv, N_HEADS, HEAD_DIM)
        v = (kv_source @ w_v.T).reshape(B, T_kv, N_HEADS, HEAD_DIM)
        scale = HEAD_DIM ** (-0.5)
        attn = jax.nn.softmax(jnp.einsum('bqhd,bkhd->bhqk', q, k) * scale, axis=-1)
        out = jnp.einsum('bhqk,bkhd->bqhd', attn, v).reshape(B, T_q, D_MODEL)
        return out @ w_o.T

    def _L0_ffn_ref(x, W_fc, ln_w, ln_b, W_proj):
        import jax, jax.numpy as jnp
        import numpy as np
        EPS = 1e-06
        LN_EPS = 1e-05

        def _absmean_core(W):
            gamma = jnp.mean(jnp.abs(W)) + EPS
            Ws = W / gamma
            Wq = jnp.sign(Ws) * jnp.minimum(jnp.round(jnp.abs(Ws)), 1.0)
            return (Wq, gamma)

        @jax.custom_vjp
        def absmean(W):
            return _absmean_core(W)[0]

        def _absmean_fwd(W):
            Wq, gamma = _absmean_core(W)
            return (Wq, gamma)

        def _absmean_bwd(gamma, g):
            return (g / gamma,)
        absmean.defvjp(_absmean_fwd, _absmean_bwd)

        def layernorm(x, w, b, eps=LN_EPS):
            mu = jnp.mean(x, axis=-1, keepdims=True)
            var = jnp.mean((x - mu) ** 2, axis=-1, keepdims=True)
            return (x - mu) * jax.lax.rsqrt(var + eps) * w + b
        h = jnp.einsum('btd,hd->bth', x, absmean(W_fc))
        h = jax.nn.gelu(h, approximate=False)
        h = layernorm(h, ln_w, ln_b)
        return jnp.einsum('bth,dh->btd', h, absmean(W_proj))
    x = x + jnp.tanh(g_xattn[0]) * _L0_xattn_ref(_layernorm(x, axis=-1), ctx_1024, L0_xattn_w_q, L0_xattn_w_k, L0_xattn_w_v, L0_xattn_w_o)
    x = x + jnp.tanh(g_ffn[0]) * _L0_ffn_ref(_layernorm(x, axis=-1), L0_ffn_W_fc, L0_ffn_ln_w, L0_ffn_ln_b, L0_ffn_W_proj)
    return x

_drawn_inputs = setup_inputs


def setup_inputs(seed=0):
    import zlib

    import numpy as np

    out = dict(_drawn_inputs(seed))
    spreads = {'L0_ffn_ln_w': (1.0, 0.2), 'L0_ffn_ln_b': (0.0, 0.1)}
    factors = {}
    for name, (base, spread) in spreads.items():
        noise = np.random.default_rng([zlib.crc32(name.encode()), seed]).standard_normal(out[name].shape)
        drawn = base * np.exp(spread * noise) if base else spread * noise
        out[name] = jnp.asarray(drawn.astype(out[name].dtype))
    for name, factor in factors.items():
        out[name] = (out[name] * factor).astype(out[name].dtype)
    return out
```

```python
import concourse.bass as bass
from concourse import mybir
from contextlib import ExitStack

P = 128
B, T, D = 2, 2048, 512
S = 77
NH, HD = 16, 32
HF = 2048
DB = D // P
HB = HF // P
NP = T // P
HS = NH * S
NJ = -(-HS // P)
HPB = P // HD
VW = HD + 1
NCHUNK = 16
CW = 2 * HF * D // P // NCHUNK
GT = 4
NG = 2 * NP // GT
LN_EPS = 1e-5
GAMMA_EPS = 1e-6

X_SCALE = 2.0 ** 11
W_SCALE = 2.0 ** 15
Q_SHIFT = 2.0 ** -20
P_SCALE = 2.0 ** 12
G_SCALE = 2.0 ** 6

QKV_ORDER = ((0, 0), (0, 1), (1, 0))


def heads_of(j):
    return P * j // S, min((P * j + P - 1) // S, NH - 1)


def rows_of(j):
    return min(P, HS - P * j)


def build(nc, x, ctx_t, wq_t, wk_t, wv_t, wo_t, w_ffn, lnw, lnb, gates, out):
    f32, f16, bf16 = mybir.dt.float32, mybir.dt.float16, mybir.dt.bfloat16
    ALU = mybir.AluOpType
    ACT = mybir.ActivationFunctionType
    AX = mybir.AxisListType
    ds = bass.ds

    x_v = x.rearrange("b (i p) d -> p i b d", p=P)
    out_v = out.rearrange("b (i p) d -> p i b d", p=P)
    blocks = "(k p) n -> p k n"

    keep = ExitStack()
    with keep:
        def sb(stack, name, shape, dt=f32):
            return stack.enter_context(nc.sbuf_tensor(name, shape, dt))

        def bank(stack, name, n=1):
            return stack.enter_context(nc.psum_tensor(name, [P, n * 512], f32))

        def sem(name):
            return keep.enter_context(nc.semaphore(name))

        xs = sb(keep, "xs", [P, NP, 2, D])
        wt = sb(keep, "wt", [P, NCHUNK, CW], f16)
        wfc = wt[:, 0:8, :].rearrange("p (k a) n -> p k (a n)", k=DB)
        wpr = wt[:, 8:16, :].rearrange("p k (a n) -> p (k a) n", a=2)
        ident = sb(keep, "ident", [P, P])
        ones = sb(keep, "ones", [P, P])
        thr = sb(keep, "thr", [P, 2, 2])
        thr_c = sb(keep, "thr_c", [P, NCHUNK, 2])
        th = sb(keep, "th", [P, 2])
        lnw_s = sb(keep, "lnw_s", [P, HB])
        lnb_s = sb(keep, "lnb_s", [P, HB])
        big = sb(keep, "big", [P, 8])
        inv = sb(keep, "inv", [P, 8])
        pad = sb(keep, "pad", [P, 1])
        pool_pad = sb(keep, "pool_pad", [P, 1])
        neg_half = sb(keep, "neg_half", [P, 8])

        att = ExitStack()
        with att:
            wq = sb(att, "wq", [P, 2, DB, D], f16)
            wo = sb(att, "wo", [P, 2, DB, D], f16)
            kd = sb(att, "kd", [P, 2, 2, HS], f16)
            vd = sb(att, "vd", [P, 2, 2, NJ, 3 * VW], f16)
            esc = sb(att, "esc", [P, 1])
            osc = sb(att, "osc", [P, 1])

            tmp = ExitStack()
            with tmp:
                wraw = [sb(tmp, f"wraw{k}", [P, DB, D]) for k in range(4)]
                wq_r, wo_r, wk_r, wv_r = wraw
                cx = sb(tmp, "cx", [P, DB, 2 * S])
                cx_rep = xs[:, 4:NP].rearrange("p i s d -> p (i s d)")[:, 0:2 * DB * HS].rearrange(
                    "p (b k n) -> p b k n", b=2, k=DB)
                kn = sb(tmp, "kn", [P, DB, 2, S])
                vr = sb(tmp, "vr", [P, 2, NJ, 3 * HD])
                vn = sb(tmp, "vn", [P, 2, NJ, 3 * VW])
                mask = sb(tmp, "mask", [P, NJ, 3 * VW])
                gate = sb(tmp, "gate", [P, 2])
                mx = sb(tmp, "mx", [P, 8])
                sc = sb(tmp, "sc", [P, 8])
                wf = [sb(tmp, f"wf{k}", [P, 2, CW]) for k in range(2)]
                asum = sb(tmp, "asum", [P, 2, 4])
                asum2 = sb(tmp, "asum2", [P, 2])
                prod = sb(tmp, "prod", [P, 4])
                k_ps = bank(tmp, "k_ps", 2)
                v_ps = [bank(tmp, f"v_ps{k}") for k in range(4)]
                g_ps = bank(tmp, "g_ps")

                s_wq, s_wo, s_wk, s_wv, s_cx, s_small, s_x0 = (sem(n) for n in (
                    "wq_loaded", "wo_loaded", "wk_loaded", "wv_loaded", "ctx_loaded", "small_loaded", "x0_loaded"))
                s_wf = [sem("wf_loaded0"), sem("wf_loaded1")]
                abs_done = sem("abs_done")
                pool_seq = sem("setup_pool_seq")
                consts = sem("consts_made")
                maxed = sem("maxed")
                big_done = sem("big_done")
                v_prod, v_out, k_prod, g_prod = sem("v_product"), sem("v_out"), sem("k_product"), sem("gamma_product")
                rep_done = sem("ctx_replicated")
                dseq = sem("setup_dve_seq")
                sc_done = sem("scales_made")
                hi_done = sem("weights_hi")
                kn_done = sem("k_scaled")
                th_done = sem("tanh_made")

                with nc.Block() as block:
                    @block.sync
                    def _(sp):
                        sp.dma_start(cx[:], ctx_t.rearrange(blocks, p=P)).then_inc(s_cx, 16)
                        sp.dma_start(wv_r[:], wv_t.rearrange(blocks, p=P)).then_inc(s_wv, 16)
                        sp.dma_start(wk_r[:], wk_t.rearrange(blocks, p=P)).then_inc(s_wk, 16)
                        sp.dma_start(wq_r[:], wq_t.rearrange(blocks, p=P)).then_inc(s_wq, 16)
                        sp.dma_start(wo_r[:], wo_t.rearrange(blocks, p=P)).then_inc(s_wo, 16)
                        sp.dma_start(lnw_s[:], lnw).then_inc(s_small, 16)
                        sp.dma_start(lnb_s[:], lnb).then_inc(s_small, 16)
                        sp.dma_start(gate[:], gates).then_inc(s_small, 16)
                        for c in range(8):
                            if c >= 2:
                                sp.wait_ge(abs_done, c - 1)
                            sp.dma_start(wf[c % 2][:], w_ffn[2 * c:2 * c + 2].rearrange("c p n -> p c n")).then_inc(s_wf[c % 2], 16)
                        for i in range(2):
                            sp.dma_start(xs[:, i], x_v[:, i]).then_inc(s_x0, 16)
                        sp.wait_ge(s_x0, 32)

                    @block.gpsimd
                    def _(pool):
                        g = nc.gpsimd
                        g.memset(ident[:], 0.0)
                        g.memset(ones[:], 1.0)
                        g.memset(neg_half[:], -0.5)
                        g.memset(mask[:], 1.0).then_inc(pool_seq, 1)
                        pool.wait_ge(pool_seq, 1)
                        g.affine_select(out=ident[:], in_=ident[:], compare_op=ALU.not_equal, fill=1.0, base=0,
                                        pattern=[[-1, P]], channel_multiplier=1).then_inc(consts, 1)
                        for j in range(NJ):
                            h0, _ = heads_of(j)
                            m = mask[:, j, :].rearrange("p (s c) -> p s c", s=3)
                            g.affine_select(out=m, in_=m, compare_op=ALU.is_ge, fill=0.0, base=P * j - S * h0,
                                            pattern=[[-S, 3], [0, VW]], channel_multiplier=1).then_inc(pool_seq, 1)
                            pool.wait_ge(pool_seq, 2 + 2 * j)
                            last = g.affine_select(out=m, in_=m, compare_op=ALU.is_ge, fill=0.0, base=S * (h0 + 1) - 1 - P * j,
                                                   pattern=[[S, 3], [0, VW]], channel_multiplier=-1)
                            last.then_inc(pool_seq, 1)
                        pool.wait_ge(pool_seq, 1 + 2 * NJ)
                        g.memset(kd[:, 0], 0.0).then_inc(consts, 1)
                        g.memset(kd[:, 1], 0.0).then_inc(consts, 1)
                        pool.wait_ge(maxed, 5)
                        g.partition_all_reduce(big[:, 0:5], mx[:, 0:5], P, bass.bass_isa.ReduceOp.absmax).then_inc(big_done, 1)

                    @block.tensor
                    def _(pe):
                        pe.wait_ge(s_cx, 16)
                        pe.wait_ge(s_wk, 16)
                        for t in range(DB):
                            for k in range(DB):
                                last = nc.tensor.matmul(k_ps[:, (t // 2) * 512 + (t % 2) * 2 * S:][:, 0:2 * S],
                                                        wk_r[:, k, t * P:(t + 1) * P], cx[:, k, :],
                                                        start=(k == 0), stop=(k == DB - 1))
                        last.then_inc(k_prod, 1)
                        pe.wait_ge(s_wv, 16)
                        for b in range(2):
                            pe.wait_ge(rep_done, 4 * (b + 1))
                            for j in range(NJ):
                                n = b * NJ + j
                                if n >= 4:
                                    pe.wait_ge(v_out, n - 3)
                                h0, h1 = heads_of(j)
                                for k in range(DB):
                                    last = nc.tensor.matmul(v_ps[n % 4][0:rows_of(j), 0:(h1 - h0 + 1) * HD],
                                                            cx_rep[:, b, k, P * j:P * j + rows_of(j)],
                                                            wv_r[:, k, h0 * HD:(h1 + 1) * HD],
                                                            start=(k == 0), stop=(k == DB - 1))
                                last.then_inc(v_prod, 1)
                        pe.wait_ge(consts, 1)
                        pe.wait_ge(dseq, 3)
                        nc.tensor.matmul(g_ps[:, 0:2], ones[:], asum2[:], start=True, stop=True).then_inc(g_prod, 1)

                    @block.scalar
                    def _(act):
                        a = nc.scalar
                        act.wait_ge(s_small, 48)
                        a.activation(th[:], gate[:], ACT.Tanh).then_inc(th_done, 1)
                        for n in range(2 * NJ):
                            b, j = divmod(n, NJ)
                            h0, h1 = heads_of(j)
                            act.wait_ge(v_prod, n + 1)
                            if n == 0:
                                act.wait_ge(dseq, 1)
                            a.copy(vr[0:rows_of(j), b, j, 0:(h1 - h0 + 1) * HD],
                                   v_ps[n % 4][0:rows_of(j), 0:(h1 - h0 + 1) * HD]).then_inc(v_out, 1)
                        for c in range(8):
                            act.wait_ge(s_wf[c % 2], 16 * (c // 2 + 1))
                            a.activation(wf[c % 2][:], wf[c % 2][:], ACT.Abs,
                                         accum_out=asum[:, c // 4, c % 4:c % 4 + 1]).then_inc(abs_done, 1)
                        act.wait_ge(sc_done, 1)
                        a.activation(wq[:, 0], wq_r[:], ACT.Copy, scale=sc[:, 0:1]).then_inc(hi_done, 1)
                        a.activation(wo[:, 0], wo_r[:], ACT.Copy, scale=sc[:, 1:2]).then_inc(hi_done, 1)

                    @block.vector
                    def _(dve):
                        v = nc.vector
                        v.memset(vr[:], 0.0).then_inc(dseq, 1)
                        dve.wait_ge(s_cx, 16)
                        for b in range(2):
                            for k in range(DB):
                                v.tensor_copy(cx_rep[:, b, k, :].rearrange("p (h s) -> p h s", h=NH),
                                              cx[:, k, b * S:(b + 1) * S].unsqueeze(1).broadcast_to([P, NH, S])).then_inc(rep_done, 1)
                        dve.wait_ge(s_wq, 16)
                        v.tensor_reduce(mx[:, 0:1], wq_r[:].rearrange("p k n -> p (k n)"), AX.X, ALU.max,
                                        apply_absolute_value=True).then_inc(maxed, 1)
                        dve.wait_ge(s_wo, 16)
                        v.tensor_reduce(mx[:, 1:2], wo_r[:].rearrange("p k n -> p (k n)"), AX.X, ALU.max,
                                        apply_absolute_value=True).then_inc(maxed, 1)
                        dve.wait_ge(s_small, 48)
                        v.tensor_reduce(mx[:, 4:5], lnw_s[:], AX.X, ALU.max, apply_absolute_value=True).then_inc(maxed, 1)
                        dve.wait_ge(k_prod, 1)
                        v.tensor_copy(kn[:].rearrange("p (a t) b s -> p a (t b s)", a=2),
                                      k_ps[:, :].rearrange("p (a n) -> p a n", a=2)[:, :, 0:4 * S]).then_inc(dseq, 1)
                        dve.wait_ge(dseq, 2)
                        v.tensor_reduce(mx[:, 2:3], kn[:].rearrange("p t b s -> p (t b s)"), AX.X, ALU.max,
                                        apply_absolute_value=True).then_inc(maxed, 1)
                        dve.wait_ge(v_out, 2 * NJ)
                        v.tensor_reduce(mx[:, 3:4], vr[:].rearrange("p b j c -> p (b j c)"), AX.X, ALU.max,
                                        apply_absolute_value=True).then_inc(maxed, 1)
                        dve.wait_ge(abs_done, 8)
                        v.tensor_reduce(asum2[:], asum[:], AX.X, ALU.add).then_inc(dseq, 1)
                        dve.wait_ge(big_done, 1)
                        v.tensor_scalar(sc[:, 0:5], big[:, 0:5], 1e-30, None, ALU.max).then_inc(dseq, 1)
                        dve.wait_ge(dseq, 4)
                        v.reciprocal(inv[:, 0:5], sc[:, 0:5]).then_inc(dseq, 1)
                        dve.wait_ge(dseq, 5)
                        v.tensor_scalar(sc[:, 0:4], inv[:, 0:4], W_SCALE, None, ALU.mult).then_inc(sc_done, 1)
                        dve.wait_ge(sc_done, 1)
                        v.tensor_scalar(kn[:], kn[:], sc[:, 2:3], None, ALU.mult).then_inc(dseq, 1)
                        v.memset(vn[:], W_SCALE).then_inc(dseq, 1)
                        dve.wait_ge(dseq, 7)
                        for b in range(2):
                            last = v.tensor_scalar(
                                vn[:, b].rearrange("p j (s c) -> p (j s) c", c=VW)[:, :, 0:HD],
                                vr[:, b].rearrange("p j (s c) -> p (j s) c", c=HD), sc[:, 3:4], None, ALU.mult)
                        last.then_inc(dseq, 1)
                        dve.wait_ge(consts, 3)
                        dve.wait_ge(dseq, 8)
                        for b in range(2):
                            last = v.tensor_tensor(vn[:, b], vn[:, b], mask[:], ALU.mult)
                        last.then_inc(dseq, 1)
                        dve.wait_ge(dseq, 9)
                        v.tensor_copy(vd[:, 0], vn[:]).then_inc(dseq, 1)
                        for q in range(HPB):
                            rows = slice(HD * q, HD * (q + 1))
                            for b in range(2):
                                last = v.tensor_copy(
                                    kd[rows, 0, b, :].rearrange("p (t q s) -> p t q s", t=DB, q=HPB)[:, :, q, :],
                                    kn[rows, :, b, :])
                        last.then_inc(dseq, 1)
                        dve.wait_ge(dseq, 11)
                        for b in range(2):
                            v.tensor_tensor(vd[:, 1, b], vn[:, b], vd[:, 0, b], ALU.subtract)
                        for q in range(HPB):
                            rows = slice(HD * q, HD * (q + 1))
                            for b in range(2):
                                v.tensor_tensor(
                                    kd[rows, 1, b, :].rearrange("p (t q s) -> p t q s", t=DB, q=HPB)[:, :, q, :],
                                    kn[rows, :, b, :],
                                    kd[rows, 0, b, :].rearrange("p (t q s) -> p t q s", t=DB, q=HPB)[:, :, q, :], ALU.subtract)
                        for n, (w, raw) in enumerate(((wq, wq_r), (wo, wo_r))):
                            dve.wait_ge(hi_done, n + 1)
                            v.scalar_tensor_tensor(w[:, 1].rearrange("p k n -> p (k n)"), raw[:].rearrange("p k n -> p (k n)"),
                                                   sc[:, n:n + 1], w[:, 0].rearrange("p k n -> p (k n)"), ALU.mult, ALU.subtract)
                        dve.wait_ge(g_prod, 1)
                        v.tensor_scalar(thr[:, 0, :], g_ps[:, 0:2], 1.0 / (HF * D), GAMMA_EPS, ALU.mult, ALU.add).then_inc(dseq, 1)
                        dve.wait_ge(dseq, 12)
                        v.tensor_scalar(thr[:, 1, :], thr[:, 0, :], -0.5, None, ALU.mult).then_inc(dseq, 1)
                        dve.wait_ge(dseq, 13)
                        v.tensor_scalar(thr[:, 0, :], thr[:, 1, :], -1.0, None, ALU.mult).then_inc(dseq, 1)
                        dve.wait_ge(dseq, 14)
                        for w in range(2):
                            last = v.tensor_copy(thr_c[:, 8 * w:8 * w + 8, :],
                                                 thr[:, :, w].unsqueeze(1).broadcast_to([P, 8, 2]))
                        dve.wait_ge(th_done, 1)
                        v.tensor_tensor(prod[:, 0:1], big[:, 0:1], big[:, 2:3], ALU.mult)
                        v.tensor_tensor(prod[:, 1:2], big[:, 1:2], big[:, 3:4], ALU.mult).then_inc(dseq, 1)
                        dve.wait_ge(dseq, 15)
                        v.tensor_scalar(esc[:], prod[:, 0:1], HD ** -0.5 / (X_SCALE * W_SCALE * Q_SHIFT * W_SCALE), None, ALU.mult)
                        v.tensor_scalar(osc[:], prod[:, 1:2], th[:, 0:1], 1.0 / (W_SCALE * W_SCALE), ALU.mult, ALU.mult)

            run = ExitStack()
            with run:
                xn = sb(run, "xn", [P, 2, D])
                st = sb(run, "st", [P, 2, 6])
                mv = sb(run, "mv", [P, 2, 2])
                ve = sb(run, "ve", [P, 2])
                rs = sb(run, "rs", [P, 2])
                xt = sb(run, "xt", [P, 2, DB, 2 * P], f16)
                q = sb(run, "q", [P, 2, DB, 2 * P], f16)
                pr = sb(run, "pr", [P, 2, HS])
                mxs = sb(run, "mxs", [P, 2, NH])
                pt = sb(run, "pt", [P, 2, 2, NJ * P], f16)
                rc = sb(run, "rc", [P, 2, NH])
                o = sb(run, "o", [P, 2, D])
                ot = sb(run, "ot", [P, 2, 2, DB, P], f16)
                wc = sb(run, "wc", [P, CW])
                wa = sb(run, "wa", [P, CW])
                wb = sb(run, "wb", [P, CW])
                tc = sb(run, "tc", [P, 2])
                sc_ps = bank(run, "sc_ps", 3)
                T0, T1, X0, V0, V1 = (bank(run, n) for n in ("T0", "T1", "X0", "V0", "V1"))
                PT_BANKS = ((T0, T1, X0), (T1, V1, T0))
                PV_BANKS = ((V0, X0), (T1, V1))
                PT_BLOCKS = ((0, 4), (4, 8), (8, NJ))
                Q_BANKS = (V1, T0)

                (x_in, xn_ready, ve_ready, rs_ready, aseq, xt_prod, xt_hi, xt_ready, q_prod, q_hi, q_ready, sc_prod, maxd, shifted,
                 expd, pt_prod, pt_hi, pt_ready, pv_prod, rcp, normed, ot_prod, ot_hi, ot_ready, o_prod, x_done,
                 w_in, w_cmp, w_done, t_cur) = (sem("a_" + n) for n in (
                    "x_in", "xn_ready", "ve_ready", "rs_ready", "dve_seq", "xt_product", "xt_hi", "xt_ready", "q_product", "q_hi",
                    "q_ready", "scores_product", "maxima", "scores_shifted", "exp_done", "pt_product", "pt_hi", "pt_ready",
                    "pv_product", "rcp_done", "o_normed", "ot_product", "ot_hi", "ot_ready", "o_product", "x_done",
                    "w_in", "w_compared", "w_done", "threshold_set"))


                with nc.Block() as block:
                    @block.sync
                    def _(sp):
                        sp.dma_start(wc[:], w_ffn[0]).then_inc(w_in, 16)

                        def load_x(i):
                            sp.dma_start(xs[:, ds(i, 1)], x_v[:, ds(i, 1)]).then_inc(x_in, 16)

                        def load_chunk(i):
                            sp.wait_ge(w_done, i)
                            sp.dma_start(wc[:], w_ffn[ds(i, 1)].rearrange("c p n -> p (c n)")).then_inc(w_in, 16)

                        load_x(2)
                        with sp.Fori(1, NP - 2) as i:
                            sp.wait_ge(x_in, 16 * i)
                            load_x(i + 2)
                            load_chunk(i)
                        load_chunk(NP - 2)
                        load_chunk(NP - 1)

                    @block.gpsimd
                    def _(pool):
                        g = nc.gpsimd

                        def carry_wait():
                            g.tensor_tensor(pool_pad[:], neg_half[:, 0:1], neg_half[:, 1:2], ALU.mult)

                        def rstd(i):
                            pool.wait_ge(ve_ready, i + 1)
                            g.tensor_tensor(rs[:], ve[:], neg_half[:, 0:2], ALU.pow).then_inc(rs_ready, 1)

                        def ternarize(i):
                            pool.wait_ge(w_in, 16 * i + 16)
                            carry_wait()
                            g.tensor_copy(tc[:], thr_c[:, ds(i, 1), :].rearrange("p a b -> p (a b)")).then_inc(t_cur, 1)
                            pool.wait_ge(t_cur, i + 1)
                            carry_wait()
                            g.tensor_scalar(wa[:], wc[:], tc[:, 0:1], None, ALU.is_gt)
                            g.tensor_scalar(wb[:], wc[:], tc[:, 1:2], None, ALU.is_lt).then_inc(w_cmp, 1)
                            pool.wait_ge(w_cmp, i + 1)
                            g.tensor_tensor(wt[:, ds(i, 1), :].rearrange("p a n -> p (a n)"), wa[:], wb[:],
                                            ALU.subtract).then_inc(w_done, 1)

                        rstd(0)
                        rstd(1)
                        with pool.Fori(0, NP - 2) as i:
                            ternarize(i)
                            rstd(i + 2)
                        for i in (NP - 2, NP - 1):
                            ternarize(i)

                    @block.tensor
                    def _(pe):
                        mm = nc.tensor.matmul

                        def transpose_x(i, s):
                            pe.wait_ge(xn_ready, 2 * i + s + 1)
                            for k in range(DB):
                                last = nc.tensor.transpose((T0, T1)[s][:, k * P:(k + 1) * P], xn[:, s, k * P:(k + 1) * P], ident[:])
                            last.then_inc(xt_prod, 1)

                        def project_q(i, half):
                            pe.wait_ge(xt_ready, 2 * i + 2)
                            for t in (2 * half, 2 * half + 1):
                                for n, (a, b) in enumerate(QKV_ORDER):
                                    for k in range(DB):
                                        last = mm(Q_BANKS[half][:, (t % 2) * 2 * P:(t % 2 + 1) * 2 * P],
                                                  wq[:, a, k, t * P:(t + 1) * P], xt[:, b, k, :],
                                                  start=(n == 0 and k == 0), stop=(n == 2 and k == DB - 1))
                            last.then_inc(q_prod, 1)

                        def scores(i, s):
                            pe.wait_ge(q_ready, 2 * i + 2)
                            for t in range(DB):
                                c0, c1 = t * HPB * S, (t + 1) * HPB * S
                                cut = [c0] + [c for c in (512, 1024) if c0 < c < c1] + [c1]
                                for lo, hi in zip(cut, cut[1:]):
                                    for n, (a, b) in enumerate(QKV_ORDER):
                                        last = mm(sc_ps[:, lo:hi], q[:, a, t, s * P:(s + 1) * P], kd[:, b, s, lo:hi],
                                                  start=(n == 0), stop=(n == 2))
                            last.then_inc(sc_prod, 1)

                        def transpose_p(i, s, final):
                            pe.wait_ge(expd, 2 * i + s + 1)
                            for c, (j0, j1) in enumerate(PT_BLOCKS):
                                if s == 1 and c > 0 and not final:
                                    pe.wait_ge(q_ready, 2 * i + 2 + c)
                                for j in range(j0, j1):
                                    last = nc.tensor.transpose(PT_BANKS[s][c][0:rows_of(j), (j - j0) * P:(j - j0 + 1) * P],
                                                               pr[:, s, P * j:P * j + rows_of(j)], ident[:])
                                last.then_inc(pt_prod, 1)

                        def weigh_v(i, s):
                            pe.wait_ge(pt_ready, 3 * (2 * i + s) + 3)
                            first = [True, True]
                            for j in range(NJ):
                                h0, h1 = heads_of(j)
                                parts = [(h0, min(h1, 7), 0)] if h0 < 8 else []
                                parts += [(max(h0, 8), h1, 1)] if h1 >= 8 else []
                                for ha, hb, side in parts:
                                    for n, (a, b) in enumerate(QKV_ORDER):
                                        final = n == 2 and (hb == 7 and j == 4 or j == NJ - 1)
                                        last = mm(PV_BANKS[s][side][:, (ha % 8) * VW:(hb % 8 + 1) * VW],
                                                  pt[0:rows_of(j), s, a, P * j:P * (j + 1)],
                                                  vd[0:rows_of(j), b, s, j, (ha - h0) * VW:(hb - h0 + 1) * VW],
                                                  start=first[side], stop=final, skip_group_check=True)
                                        first[side] = False
                            last.then_inc(pv_prod, 1)

                        def transpose_o(i, s):
                            pe.wait_ge(normed, 2 * i + s + 1)
                            for k in range(DB):
                                last = nc.tensor.transpose(X0[:, k * P:(k + 1) * P], o[:, s, k * P:(k + 1) * P], ident[:])
                            last.then_inc(ot_prod, 1)

                        def project_o(i, s):
                            pe.wait_ge(ot_ready, 2 * i + s + 1)
                            for n, (a, b) in enumerate(QKV_ORDER):
                                for k in range(DB):
                                    last = mm(V0[:, :], ot[:, s, a, k, :], wo[:, b, k, :],
                                              start=(n == 0 and k == 0), stop=(n == 2 and k == DB - 1))
                            last.then_inc(o_prod, 1)

                        def one_pair(i, first=False, final=False):
                            if not first:
                                pe.wait_ge(shifted, 2 * i)
                            scores(i, 0)
                            if not first:
                                transpose_o(i - 1, 1)
                            if not final:
                                transpose_x(i + 1, 0)
                                transpose_x(i + 1, 1)
                            if not first:
                                pe.wait_ge(x_done, 2 * i - 1)
                                project_o(i - 1, 1)
                            pe.wait_ge(shifted, 2 * i + 1)
                            scores(i, 1)
                            if not final:
                                pe.wait_ge(xt_ready, 2 * i + 4)
                            transpose_p(i, 0, final)
                            if not final:
                                project_q(i + 1, 0)
                            if not first:
                                pe.wait_ge(x_done, 2 * i)
                            weigh_v(i, 0)
                            if not final:
                                project_q(i + 1, 1)
                            transpose_p(i, 1, final)
                            transpose_o(i, 0)
                            weigh_v(i, 1)
                            project_o(i, 0)

                        transpose_x(0, 0)
                        transpose_x(0, 1)
                        project_q(0, 0)
                        project_q(0, 1)
                        one_pair(0, first=True)
                        with pe.Fori(1, NP - 1) as i:
                            one_pair(i)
                        one_pair(NP - 1, final=True)
                        transpose_o(NP - 1, 1)
                        pe.wait_ge(x_done, 2 * NP - 1)
                        project_o(NP - 1, 1)

                    @block.scalar
                    def _(act):
                        a = nc.scalar

                        def x_high(i, s):
                            act.wait_ge(xt_prod, 2 * i + s + 1)
                            a.copy(xt[:, 0, :, s * P:(s + 1) * P],
                                   (T0, T1)[s][:, :].rearrange("p (k n) -> p k n", k=DB)).then_inc(xt_hi, 1)

                        def q_high(i, half):
                            act.wait_ge(q_prod, 2 * i + half + 1)
                            a.mul(q[:, 0, 2 * half:2 * half + 2, :],
                                  Q_BANKS[half][:, :].rearrange("p (t n) -> p t n", t=2), Q_SHIFT).then_inc(q_hi, 1)

                        def exp(i, s):
                            act.wait_ge(shifted, 2 * i + s + 1)
                            a.activation(pr[:, s], pr[:, s], ACT.Exp, scale=esc[:]).then_inc(expd, 1)

                        def p_high(i, s):
                            for c, (j0, j1) in enumerate(PT_BLOCKS):
                                act.wait_ge(pt_prod, 3 * (2 * i + s) + c + 1)
                                for lo, hi, rows in ((j0, j1, P),) if j1 < NJ else ((j0, j1 - 1, P), (j1 - 1, j1, rows_of(NJ - 1))):
                                    last = a.mul(pt[0:rows, s, 0, P * lo:P * hi],
                                                 PT_BANKS[s][c][0:rows, P * (lo - j0):P * (hi - j0)], P_SCALE)
                                last.then_inc(pt_hi, 1)

                        def o_high(i, s):
                            act.wait_ge(ot_prod, 2 * i + s + 1)
                            a.mul(ot[:, s, 0].rearrange("p k n -> p (k n)"), X0[:, :], W_SCALE).then_inc(ot_hi, 1)

                        def one_pair(i, first=False, final=False):
                            if not first:
                                o_high(i - 1, 1)
                            if not final:
                                x_high(i + 1, 0)
                                x_high(i + 1, 1)
                            exp(i, 0)
                            p_high(i, 0)
                            if not final:
                                q_high(i + 1, 0)
                            exp(i, 1)
                            if not final:
                                q_high(i + 1, 1)
                            p_high(i, 1)
                            o_high(i, 0)

                        x_high(0, 0)
                        x_high(0, 1)
                        q_high(0, 0)
                        q_high(0, 1)
                        one_pair(0, first=True)
                        with act.Fori(1, NP - 1) as i:
                            one_pair(i)
                        one_pair(NP - 1, final=True)
                        o_high(NP - 1, 1)

                    @block.vector
                    def _(dve):
                        v = nc.vector

                        def norm_x(i):
                            for s in range(2):
                                last = v.bn_stats(st[:, s, :], xs[:, ds(i, 1), s, :].rearrange("p a n -> p (a n)"))
                            last.then_inc(aseq, 1)
                            dve.wait_ge(aseq, 2 * i + 1)
                            v.memset(pad[:], 0.0)
                            for s in range(2):
                                last = v.bn_aggr(mv[:, s, :], st[:, s, :])
                            last.then_inc(aseq, 1)
                            dve.wait_ge(aseq, 2 * i + 2)
                            v.tensor_scalar(ve[:], mv[:, :, 1], LN_EPS, X_SCALE ** -2, ALU.add, ALU.mult).then_inc(ve_ready, 1)

                        def scale_x(i):
                            dve.wait_ge(rs_ready, i + 1)
                            for s in range(2):
                                last = v.tensor_scalar(xn[:, s, :], xs[:, ds(i, 1), s, :].rearrange("p a n -> p (a n)"),
                                                       mv[:, s, 0:1], rs[:, s:s + 1], ALU.subtract, ALU.mult)
                                last.then_inc(xn_ready, 1)

                        def x_low(i, s):
                            dve.wait_ge(xt_hi, 2 * i + s + 1)
                            v.tensor_tensor(xt[:, 1, :, s * P:(s + 1) * P],
                                            (T0, T1)[s][:, :].rearrange("p (k n) -> p k n", k=DB),
                                            xt[:, 0, :, s * P:(s + 1) * P], ALU.subtract).then_inc(xt_ready, 1)

                        def q_low(i, half):
                            dve.wait_ge(q_hi, 2 * i + half + 1)
                            v.scalar_tensor_tensor(q[:, 1, 2 * half:2 * half + 2, :].rearrange("p t n -> p (t n)"),
                                                   Q_BANKS[half][:, :], Q_SHIFT,
                                                   q[:, 0, 2 * half:2 * half + 2, :].rearrange("p t n -> p (t n)"),
                                                   ALU.mult, ALU.subtract).then_inc(q_ready, 1)

                        def shift_scores(i, s):
                            dve.wait_ge(sc_prod, 2 * i + s + 1)
                            grid = sc_ps[:, 0:HS].rearrange("p (h k) -> p h k", h=NH)
                            v.tensor_reduce(mxs[:, s, :], grid, AX.X, ALU.max).then_inc(maxd, 1)
                            dve.wait_ge(maxd, 2 * i + s + 1)
                            v.tensor_tensor(pr[:, s, :].rearrange("p (h k) -> p h k", h=NH), grid,
                                            mxs[:, s, :].unsqueeze(2).broadcast_to([P, NH, S]), ALU.subtract).then_inc(shifted, 1)

                        def p_low(i, s):
                            for c, (j0, j1) in enumerate(PT_BLOCKS):
                                dve.wait_ge(pt_hi, 3 * (2 * i + s) + c + 1)
                                for lo, hi, rows in ((j0, j1, P),) if j1 < NJ else ((j0, j1 - 1, P), (j1 - 1, j1, rows_of(NJ - 1))):
                                    last = v.scalar_tensor_tensor(pt[0:rows, s, 1, P * lo:P * hi],
                                                                  PT_BANKS[s][c][0:rows, P * (lo - j0):P * (hi - j0)], P_SCALE,
                                                                  pt[0:rows, s, 0, P * lo:P * hi], ALU.mult, ALU.subtract)
                                last.then_inc(pt_ready, 1)

                        def norm_o(i, s):
                            dve.wait_ge(pv_prod, 2 * i + s + 1)
                            for side in range(2):
                                grid = PV_BANKS[s][side][:, 0:8 * VW].rearrange("p (h c) -> p h c", h=8)
                                last = v.reciprocal(rc[:, s, 8 * side:8 * side + 8], grid[:, :, HD])
                            last.then_inc(rcp, 1)
                            dve.wait_ge(rcp, 2 * i + s + 1)
                            for side in range(2):
                                grid = PV_BANKS[s][side][:, 0:8 * VW].rearrange("p (h c) -> p h c", h=8)
                                last = v.tensor_tensor(
                                    o[:, s, side * D // 2:(side + 1) * D // 2].rearrange("p (h c) -> p h c", h=8), grid[:, :, 0:HD],
                                    rc[:, s, 8 * side:8 * side + 8].unsqueeze(2).broadcast_to([P, 8, HD]), ALU.mult)
                            last.then_inc(normed, 1)

                        def o_low(i, s):
                            dve.wait_ge(ot_hi, 2 * i + s + 1)
                            v.scalar_tensor_tensor(ot[:, s, 1].rearrange("p k n -> p (k n)"), X0[:, :], W_SCALE,
                                                   ot[:, s, 0].rearrange("p k n -> p (k n)"),
                                                   ALU.mult, ALU.subtract).then_inc(ot_ready, 1)

                        def add_branch(i, s):
                            dve.wait_ge(o_prod, 2 * i + s + 1)
                            tile = xs[:, ds(i, 1), s, :].rearrange("p a n -> p (a n)")
                            v.scalar_tensor_tensor(tile, V0[:, :], osc[:], tile, ALU.mult, ALU.add).then_inc(x_done, 1)

                        def one_pair(i, first=False, final=False, ahead=True):
                            shift_scores(i, 0)
                            if not first:
                                o_low(i - 1, 1)
                            if not final:
                                x_low(i + 1, 0)
                                x_low(i + 1, 1)
                            if not first:
                                add_branch(i - 1, 1)
                            shift_scores(i, 1)
                            if ahead:
                                dve.wait_ge(x_in, 16 * i + 16)
                                norm_x(i + 2)
                            p_low(i, 0)
                            if not final:
                                q_low(i + 1, 0)
                            norm_o(i, 0)
                            if not final:
                                q_low(i + 1, 1)
                            p_low(i, 1)
                            o_low(i, 0)
                            if ahead:
                                scale_x(i + 2)
                            norm_o(i, 1)
                            add_branch(i, 0)

                        norm_x(0)
                        scale_x(0)
                        x_low(0, 0)
                        x_low(0, 1)
                        norm_x(1)
                        scale_x(1)
                        q_low(0, 0)
                        q_low(0, 1)
                        one_pair(0, first=True)
                        with dve.Fori(1, NP - 2) as i:
                            one_pair(i)
                        one_pair(NP - 2, ahead=False)
                        one_pair(NP - 1, final=True, ahead=False)
                        o_low(NP - 1, 1)
                        add_branch(NP - 1, 1)

        ffn = ExitStack()
        with ffn:
            NT = 2 * NP
            xt_all = xs[:].rearrange("p i s d -> p (i s) d")
            xn = sb(ffn, "xn2", [P, GT, D])
            st = sb(ffn, "st2", [P, GT, 6])
            mv = sb(ffn, "mv2", [P, GT, 2])
            ve = sb(ffn, "ve2", [P, GT])
            rs = sb(ffn, "rs2", [P, GT])
            xt = sb(ffn, "xt2", [P, 2, DB, GT * P], f16)
            gf = sb(ffn, "gf", [P, 4, GT * P])
            sq = sb(ffn, "sq", [P, 4, GT * P])
            s12 = sb(ffn, "s12", [P, 2, GT * P])
            gw = sb(ffn, "gw", [P, 2, HB, GT * P], f16)
            zero = sb(ffn, "zero", [P, GT * P])
            wsc = sb(ffn, "wsc", [P, HB])
            parts = sb(ffn, "parts", [P, HB, 6], bf16)
            rest = sb(ffn, "rest", [P, 2, HB])
            colsum = sb(ffn, "colsum", [6, D])
            pick = sb(ffn, "pick", [6, 2, P])
            cw = sb(ffn, "cw", [P, D])
            cb = sb(ffn, "cb", [P, D])
            fsc = sb(ffn, "fsc", [P, 1])
            negm = sb(ffn, "negm", [P, GT])
            m2 = sb(ffn, "m2", [P, GT])
            ge = sb(ffn, "ge", [P, GT])
            grs = sb(ffn, "grs", [P, GT])
            gr = sb(ffn, "gr", [P, GT])
            t1 = sb(ffn, "t1", [P, D])
            t2 = sb(ffn, "t2", [P, D])
            ob = sb(ffn, "ob", [P, 2, D])
            Z = [bank(ffn, f"Z{k}") for k in range(4)]
            R = [bank(ffn, f"R{k}") for k in range(2)]
            XB = bank(ffn, "XB")
            SB = bank(ffn, "SB")

            (pieces, picked, fseq, c6, c6_out, cwb, c_done, gseq, ve_ready, rs_ready, xn_ready, xt_prod, xt_hi, xt_ready,
             z_prod, gelu_done, sq_done, s1_done, s2_done, gw_hi, gw_ready, r_prod, st_prod, sseq, ge_ready, grs_ready,
             r_read, fin, ob_ready) = (sem("f_" + n) for n in (
                "pieces_made", "pick_made", "dve_seq", "column_sums", "column_sums_out", "column_sums_bcast", "consts_done",
                "ln_seq", "ve_ready", "rs_ready", "xn_ready", "xt_product", "xt_hi", "xt_ready", "z_product", "gelu_done",
                "sq_done", "s1_done", "s2_done", "gw_hi", "gw_ready", "r_product", "stats_product", "stats_seq", "ge_ready",
                "grs_ready", "r_read", "final_seq", "ob_ready"))
            stored = [sem("f_stored0"), sem("f_stored1")]


            with nc.Block() as block:
                @block.sync
                def _(sp):
                    with sp.Fori(0, NG) as g:
                        for tt in range(GT):
                            sp.wait_ge(ob_ready, GT * g + tt + 1)
                            sp.dma_start(out_v[:, ds(2 * g + tt // 2, 1), tt % 2, :],
                                         ob[:, tt % 2:tt % 2 + 1, :]).then_inc(stored[tt % 2], 16)
                    for k in range(2):
                        sp.wait_ge(stored[k], 16 * NT // 2)

                @block.gpsimd
                def _(pool):
                    g_ = nc.gpsimd
                    g_.memset(zero[:], 0.0)
                    g_.memset(pick[:], 1.0).then_inc(picked, 1)
                    pool.wait_ge(picked, 1)
                    g_.affine_select(out=pick[:, 0, :], in_=pick[:, 0, :], compare_op=ALU.is_ge, fill=0.0, base=2,
                                     pattern=[[0, P]], channel_multiplier=-1)
                    g_.affine_select(out=pick[:, 1, :], in_=pick[:, 1, :], compare_op=ALU.is_ge, fill=0.0, base=-3,
                                     pattern=[[0, P]], channel_multiplier=1).then_inc(picked, 1)

                    def rstd(g):
                        pool.wait_ge(ve_ready, g + 1)
                        g_.tensor_tensor(rs[:], ve[:], neg_half[:, 0:GT], ALU.pow).then_inc(rs_ready, 1)

                    def sums(g, h):
                        pool.wait_ge(gelu_done, HB * g + h + 1)
                        if h == 0:
                            g_.tensor_tensor(s12[:, 0], gf[:, 0], zero[:], ALU.add).then_inc(s1_done, 1)
                        else:
                            pool.wait_ge(s1_done, HB * g + h)
                            g_.tensor_tensor(s12[:, 0], s12[:, 0], gf[:, h % 4], ALU.add).then_inc(s1_done, 1)
                        pool.wait_ge(sq_done, HB * g + h + 1)
                        if h == 0:
                            g_.tensor_tensor(s12[:, 1], sq[:, 0], zero[:], ALU.add).then_inc(s2_done, 1)
                        else:
                            pool.wait_ge(s2_done, HB * g + h)
                            g_.tensor_tensor(s12[:, 1], s12[:, 1], sq[:, h % 4], ALU.add).then_inc(s2_done, 1)

                    def group(g, final=False):
                        for h in range(HB):
                            sums(g, h)
                            if h == 6 and not final:
                                rstd(g + 1)
                        pool.wait_ge(ge_ready, g + 1)
                        g_.tensor_tensor(grs[:], ge[:], neg_half[:, 0:GT], ALU.pow).then_inc(grs_ready, 1)

                    rstd(0)
                    with pool.Fori(0, NG - 1) as g:
                        group(g)
                    group(NG - 1, final=True)

                @block.tensor
                def _(pe):
                    mm = nc.tensor.matmul

                    def transpose_x(g, tt, first=False):
                        pe.wait_ge(xn_ready, GT * g + tt + 1)
                        if not (first and tt == 0):
                            pe.wait_ge(xt_ready, GT * g + tt)
                        for k in range(DB):
                            last = nc.tensor.transpose(XB[:, k * P:(k + 1) * P], xn[:, tt, k * P:(k + 1) * P], ident[:])
                        last.then_inc(xt_prod, 1)

                    def up(g, h, first):
                        if not (first and h < 4):
                            pe.wait_ge(gelu_done, HB * g + h - 3)
                        for k in range(DB):
                            for a in range(2):
                                last = mm(Z[h % 4][:, :], wfc[:, k, h * P:(h + 1) * P], xt[:, a, k, :],
                                          start=(k == 0 and a == 0), stop=(k == DB - 1 and a == 1))
                        last.then_inc(z_prod, 1)

                    def down(g, tt, first):
                        if not (first and tt < 2):
                            pe.wait_ge(r_read, GT * g + tt - 1)
                        for h in range(HB):
                            if tt == 0:
                                pe.wait_ge(gw_ready, HB * g + h + 1)
                            for a in range(2):
                                last = mm(R[tt % 2][:, :], gw[:, a, h, tt * P:(tt + 1) * P], wpr[:, h, :],
                                          start=(h == 0 and a == 0), stop=(h == HB - 1 and a == 1))
                        last.then_inc(r_prod, 1)

                    def stats(g):
                        pe.wait_ge(s1_done, HB * g + HB)
                        pe.wait_ge(s2_done, HB * g + HB)
                        for tt in range(GT):
                            for k in range(2):
                                last = mm(SB[:, 2 * tt + k:2 * tt + k + 1], s12[:, k, tt * P:(tt + 1) * P], ones[:, 0:1],
                                          start=True, stop=True)
                        last.then_inc(st_prod, 1)

                    def group(g, first=False, final=False):
                        pe.wait_ge(xt_ready, GT * g + GT)
                        for h in range(HB):
                            up(g, h, first)
                        for tt in range(GT):
                            down(g, tt, first)
                            if tt == 0:
                                stats(g)
                            if not final:
                                transpose_x(g + 1, tt)

                    for tt in range(GT):
                        transpose_x(0, tt, first=True)
                    pe.wait_ge(pieces, 1)
                    for h in range(HB):
                        last = mm(R[0][0:6, :], parts[:, h, :], wpr[:, h, :], start=(h == 0), stop=(h == HB - 1))
                    last.then_inc(c6, 1)
                    pe.wait_ge(c6_out, 1)
                    pe.wait_ge(picked, 2)
                    mm(R[1][:, :], pick[:, 0, :], colsum[:], start=True, stop=True)
                    mm(SB[:, :], pick[:, 1, :], colsum[:], start=True, stop=True).then_inc(cwb, 1)
                    pe.wait_ge(c_done, 1)
                    group(0, first=True)
                    with pe.Fori(1, NG - 1) as g:
                        group(g)
                    group(NG - 1, final=True)

                @block.scalar
                def _(act):
                    a_ = nc.scalar

                    def x_high(g, tt):
                        act.wait_ge(xt_prod, GT * g + tt + 1)
                        a_.copy(xt[:, 0, :, tt * P:(tt + 1) * P], XB[:, :].rearrange("p (k n) -> p k n", k=DB)).then_inc(xt_hi, 1)

                    def square(g, h, first):
                        act.wait_ge(gelu_done, HB * g + h + 1)
                        if not (first and h < 4):
                            act.wait_ge(s2_done, HB * g + h - 3)
                        a_.activation(sq[:, h % 4], gf[:, h % 4], ACT.Square).then_inc(sq_done, 1)

                    def gelu(g, h, first):
                        act.wait_ge(z_prod, HB * g + h + 1)
                        if not (first and h < 4):
                            act.wait_ge(gw_ready, HB * g + h - 3)
                            act.wait_ge(s1_done, HB * g + h - 3)
                        a_.activation(gf[:, h % 4], Z[h % 4][:, :], ACT.Gelu, scale=1.0 / X_SCALE).then_inc(gelu_done, 1)

                    def group(g, first=False, final=False):
                        for h in range(HB):
                            gelu(g, h, first)
                            if h:
                                square(g, h - 1, first)
                        square(g, HB - 1, first)
                        if not final:
                            for tt in range(GT):
                                x_high(g + 1, tt)

                    for tt in range(GT):
                        x_high(0, tt)
                    group(0, first=True)
                    with act.Fori(1, NG - 1) as g:
                        group(g)
                    group(NG - 1, final=True)

                @block.vector
                def _(dve):
                    v = nc.vector

                    def norm_x(g):
                        for tt in range(GT):
                            last = v.bn_stats(st[:, tt, :], xt_all[:, ds(GT * g + tt, 1), :].rearrange("p a n -> p (a n)"))
                        last.then_inc(gseq, 1)
                        dve.wait_ge(gseq, 2 * g + 1)
                        v.memset(pad[:], 0.0)
                        for tt in range(GT):
                            last = v.bn_aggr(mv[:, tt, :], st[:, tt, :])
                        last.then_inc(gseq, 1)
                        dve.wait_ge(gseq, 2 * g + 2)
                        v.tensor_scalar(ve[:], mv[:, :, 1], LN_EPS, X_SCALE ** -2, ALU.add, ALU.mult).then_inc(ve_ready, 1)

                    def scale_x(g):
                        dve.wait_ge(rs_ready, g + 1)
                        for tt in range(GT):
                            v.tensor_scalar(xn[:, tt, :], xt_all[:, ds(GT * g + tt, 1), :].rearrange("p a n -> p (a n)"),
                                            mv[:, tt, 0:1], rs[:, tt:tt + 1], ALU.subtract, ALU.mult).then_inc(xn_ready, 1)

                    def x_low(g, tt):
                        dve.wait_ge(xt_hi, GT * g + tt + 1)
                        v.tensor_tensor(xt[:, 1, :, tt * P:(tt + 1) * P], XB[:, :].rearrange("p (k n) -> p k n", k=DB),
                                        xt[:, 0, :, tt * P:(tt + 1) * P], ALU.subtract).then_inc(xt_ready, 1)

                    def split_g(g, h, first):
                        dve.wait_ge(gelu_done, HB * g + h + 1)
                        if h == 0 and not first:
                            dve.wait_ge(r_prod, GT * g)
                        v.tensor_scalar(gw[:, 0, h, :], gf[:, h % 4], wsc[:, h:h + 1], None, ALU.mult).then_inc(gw_hi, 1)
                        dve.wait_ge(gw_hi, HB * g + h + 1)
                        v.scalar_tensor_tensor(gw[:, 1, h, :], gf[:, h % 4], wsc[:, h:h + 1], gw[:, 0, h, :],
                                               ALU.mult, ALU.subtract).then_inc(gw_ready, 1)

                    def moments(g):
                        dve.wait_ge(st_prod, g + 1)
                        pair = SB[:, 0:2 * GT].rearrange("p (t k) -> p t k", k=2)
                        v.tensor_scalar(negm[:], pair[:, :, 0], -1.0 / HF, None, ALU.mult).then_inc(sseq, 1)
                        dve.wait_ge(sseq, 3 * g + 1)
                        v.tensor_tensor(m2[:], negm[:], negm[:], ALU.mult).then_inc(sseq, 1)
                        dve.wait_ge(sseq, 3 * g + 2)
                        v.scalar_tensor_tensor(ge[:], pair[:, :, 1], 1.0 / HF, m2[:], ALU.mult, ALU.subtract).then_inc(sseq, 1)
                        dve.wait_ge(sseq, 3 * g + 3)
                        v.tensor_scalar(ge[:], ge[:], 0.0, LN_EPS, ALU.max, ALU.add).then_inc(ge_ready, 1)
                        dve.wait_ge(grs_ready, g + 1)
                        v.tensor_scalar(gr[:], grs[:], fsc[:], None, ALU.mult).then_inc(fin, 1)

                    def finish(g, tt, first):
                        n = GT * g + tt
                        dve.wait_ge(r_prod, n + 1)
                        if tt == 0:
                            dve.wait_ge(fin, 5 * g + 1)
                        v.scalar_tensor_tensor(t1[:], cw[:], negm[:, tt:tt + 1], R[tt % 2][:, :], ALU.mult, ALU.add).then_inc(r_read, 1)
                        dve.wait_ge(r_read, n + 1)
                        v.scalar_tensor_tensor(t2[:], t1[:], gr[:, tt:tt + 1],
                                               xt_all[:, ds(n, 1), :].rearrange("p a n -> p (a n)"), ALU.mult, ALU.add).then_inc(fin, 1)
                        dve.wait_ge(fin, 5 * g + tt + 2)
                        if not (first and tt < 2):
                            dve.wait_ge(stored[tt % 2], 16 * (2 * g + tt // 2))
                        v.tensor_tensor(ob[:, tt % 2, :], t2[:], cb[:], ALU.add).then_inc(ob_ready, 1)

                    def group(g, first=False, final=False):
                        for h in range(HB):
                            split_g(g, h, first)
                            if h == 3 and not final:
                                norm_x(g + 1)
                            if h == 9 and not final:
                                scale_x(g + 1)
                        moments(g)
                        for tt in range(GT):
                            if not final:
                                x_low(g + 1, tt)
                            finish(g, tt, first)

                    norm_x(0)
                    scale_x(0)
                    v.tensor_scalar(wsc[:], lnw_s[:], inv[:, 4:5], G_SCALE, ALU.mult, ALU.mult).then_inc(fseq, 1)
                    dve.wait_ge(fseq, 1)
                    v.tensor_copy(parts[:, :, 0], wsc[:])
                    v.tensor_copy(parts[:, :, 3], lnb_s[:]).then_inc(fseq, 1)
                    dve.wait_ge(fseq, 2)
                    v.tensor_tensor(rest[:, 0, :], wsc[:], parts[:, :, 0], ALU.subtract)
                    v.tensor_tensor(rest[:, 1, :], lnb_s[:], parts[:, :, 3], ALU.subtract).then_inc(fseq, 1)
                    dve.wait_ge(fseq, 3)
                    v.tensor_copy(parts[:, :, 1], rest[:, 0, :])
                    v.tensor_copy(parts[:, :, 4], rest[:, 1, :]).then_inc(fseq, 1)
                    dve.wait_ge(fseq, 4)
                    v.tensor_tensor(parts[:, :, 2], rest[:, 0, :], parts[:, :, 1], ALU.subtract)
                    v.tensor_tensor(parts[:, :, 5], rest[:, 1, :], parts[:, :, 4], ALU.subtract).then_inc(pieces, 1)
                    v.tensor_scalar(fsc[:], big[:, 4:5], th[:, 1:2], 1.0 / G_SCALE, ALU.mult, ALU.mult)
                    for tt in range(GT):
                        x_low(0, tt)
                    dve.wait_ge(c6, 1)
                    v.tensor_copy(colsum[:], R[0][0:6, :]).then_inc(c6_out, 1)
                    dve.wait_ge(cwb, 1)
                    v.tensor_copy(cw[:], R[1][:, :])
                    v.tensor_scalar(cb[:], SB[:, :], th[:, 1:2], None, ALU.mult).then_inc(c_done, 1)
                    group(0, first=True)
                    with dve.Fori(1, NG - 1) as g:
                        group(g)
                    group(NG - 1, final=True)


def kernel(**inputs):
    import numpy as np
    import concourse.bacc as bacc
    from concourse.bass_utils import run_bass_kernel_spmd

    def a(name):
        return np.asarray(inputs[name])

    def turned(name):
        return np.ascontiguousarray(a(name).T)

    fc = turned("L0_ffn_W_fc").reshape(DB, P, 2, CW).transpose(0, 2, 1, 3).reshape(8, P, CW)
    proj = turned("L0_ffn_W_proj").reshape(8, 2, P, D).transpose(0, 2, 1, 3).reshape(8, P, CW)
    arrays = {
        "x": np.ascontiguousarray(a("x")),
        "ctx_t": np.ascontiguousarray(a("ctx_1024").reshape(B * S, D).T),
        "wq_t": turned("L0_xattn_w_q"), "wk_t": turned("L0_xattn_w_k"),
        "wv_t": turned("L0_xattn_w_v"), "wo_t": turned("L0_xattn_w_o"),
        "w_ffn": np.ascontiguousarray(np.concatenate([fc, proj])),
        "lnw": np.ascontiguousarray(a("L0_ffn_ln_w").reshape(HB, P).T),
        "lnb": np.ascontiguousarray(a("L0_ffn_ln_b").reshape(HB, P).T),
        "gates": np.ascontiguousarray(np.broadcast_to(np.stack([a("g_xattn")[0], a("g_ffn")[0]]), (P, 2))),
    }
    nc = bacc.Bacc("TRN2", target_bir_lowering=False, num_devices=1)
    args = [nc.dram_tensor(n, v.shape, mybir.dt.from_np(v.dtype), kind="ExternalInput").ap() for n, v in arrays.items()]
    out = nc.dram_tensor("out", (B, T, D), mybir.dt.float32, kind="ExternalOutput").ap()
    build(nc, *args, out)
    r = run_bass_kernel_spmd(nc, [arrays], core_ids=[0])
    return r.results[0]["out"]
```

```python
import concourse.bass as bass
from concourse import mybir
from contextlib import ExitStack

P = 128
B, T, D = 2, 2048, 512
S = 77
NH, HD = 16, 32
HF = 2048
DB = D // P
HB = HF // P
NP = T // P
HS = NH * S
NJ = -(-HS // P)
HPB = P // HD
VW = HD + 1
NCHUNK = 16
CW = 2 * HF * D // P // NCHUNK
GT = 4
NG = 2 * NP // GT
LN_EPS = 1e-5
GAMMA_EPS = 1e-6

X_SCALE = 2.0 ** 11
W_SCALE = 2.0 ** 15
Q_SHIFT = 2.0 ** -20
P_SCALE = 2.0 ** 12
G_SCALE = 2.0 ** 6

QKV_ORDER = ((0, 0), (0, 1), (1, 0))


def heads_of(j):
    return P * j // S, min((P * j + P - 1) // S, NH - 1)


def rows_of(j):
    return min(P, HS - P * j)


def build(nc, x, ctx_t, wq_t, wk_t, wv_t, wo_t, w_ffn, lnw, lnb, gates, out):
    f32, f16, bf16 = mybir.dt.float32, mybir.dt.float16, mybir.dt.bfloat16
    ALU = mybir.AluOpType
    ACT = mybir.ActivationFunctionType
    AX = mybir.AxisListType
    ds = bass.ds

    x_v = x.rearrange("b (i p) d -> p i b d", p=P)
    out_v = out.rearrange("b (i p) d -> p i b d", p=P)
    blocks = "(k p) n -> p k n"

    keep = ExitStack()
    with keep:
        def sb(stack, name, shape, dt=f32):
            return stack.enter_context(nc.sbuf_tensor(name, shape, dt))

        def bank(stack, name, n=1):
            return stack.enter_context(nc.psum_tensor(name, [P, n * 512], f32))

        def sem(name):
            return keep.enter_context(nc.semaphore(name))

        xs = sb(keep, "xs", [P, NP, 2, D])
        wt = sb(keep, "wt", [P, NCHUNK, CW], f16)
        wfc = wt[:, 0:8, :].rearrange("p (k a) n -> p k (a n)", k=DB)
        wpr = wt[:, 8:16, :].rearrange("p k (a n) -> p (k a) n", a=2)
        ident = sb(keep, "ident", [P, P])
        ones = sb(keep, "ones", [P, P])
        thr = sb(keep, "thr", [P, 2, 2])
        thr_c = sb(keep, "thr_c", [P, NCHUNK, 2])
        th = sb(keep, "th", [P, 2])
        lnw_s = sb(keep, "lnw_s", [P, HB])
        lnb_s = sb(keep, "lnb_s", [P, HB])
        big = sb(keep, "big", [P, 8])
        inv = sb(keep, "inv", [P, 8])
        pad = sb(keep, "pad", [P, 1])
        pool_pad = sb(keep, "pool_pad", [P, 1])
        xn = sb(keep, "xn", [P, 2, D])
        st = sb(keep, "st", [P, 2, 6])
        mv = sb(keep, "mv", [P, 2, 2])
        ve = sb(keep, "ve", [P, 2])
        rs = sb(keep, "rs", [P, 2])
        NT = 2 * NP
        xs_tiles = xs[:].rearrange("p i s d -> p (i s) d")
        g_xn = sb(keep, "g_xn", [P, GT, D])
        g_st = sb(keep, "g_st", [P, GT, 6])
        g_mv = sb(keep, "g_mv", [P, GT, 2])
        g_ve = sb(keep, "g_ve", [P, GT])
        g_xt = sb(keep, "g_xt", [P, 2, DB, GT * P], f16)
        g_rs = sb(keep, "g_rs", [P, GT])
        aseq, ve_ready, rs_ready, xn_ready = (sem("a_" + n) for n in ("ln_seq", "ve_ready", "rs_ready", "xn_ready"))
        gseq, g_ve_ready, g_rs_ready, g_xn_ready, g_xt_prod, g_xt_hi, g_xt_ready = (sem("f_" + n) for n in (
            "ln_seq", "ve_ready", "rs_ready", "xn_ready", "xt_product", "xt_hi", "xt_ready"))

        def norm_x(i):
            for s in range(2):
                last = nc.vector.bn_stats(st[:, s, :], xs[:, ds(i, 1), s, :].rearrange("p a n -> p (a n)"))
            last.then_inc(aseq, 1)
            nc.vector.wait_ge(aseq, 2 * i + 1)
            nc.vector.memset(pad[:], 0.0)
            for s in range(2):
                last = nc.vector.bn_aggr(mv[:, s, :], st[:, s, :])
            last.then_inc(aseq, 1)
            nc.vector.wait_ge(aseq, 2 * i + 2)
            nc.vector.tensor_scalar(ve[:], mv[:, :, 1], LN_EPS, X_SCALE ** -2, ALU.add, ALU.mult).then_inc(ve_ready, 1)

        def scale_x(i):
            nc.vector.wait_ge(rs_ready, i + 1)
            for s in range(2):
                nc.vector.tensor_scalar(xn[:, s, :], xs[:, ds(i, 1), s, :].rearrange("p a n -> p (a n)"),
                                        mv[:, s, 0:1], rs[:, s:s + 1], ALU.subtract, ALU.mult).then_inc(xn_ready, 1)

        def norm_group(g):
            for tt in range(GT):
                last = nc.vector.bn_stats(g_st[:, tt, :], xs_tiles[:, ds(GT * g + tt, 1), :].rearrange("p a n -> p (a n)"))
            last.then_inc(gseq, 1)
            nc.vector.wait_ge(gseq, 2 * g + 1)
            nc.vector.memset(pad[:], 0.0)
            for tt in range(GT):
                last = nc.vector.bn_aggr(g_mv[:, tt, :], g_st[:, tt, :])
            last.then_inc(gseq, 1)
            nc.vector.wait_ge(gseq, 2 * g + 2)
            nc.vector.tensor_scalar(g_ve[:], g_mv[:, :, 1], LN_EPS, X_SCALE ** -2, ALU.add, ALU.mult).then_inc(g_ve_ready, 1)

        def scale_group(g):
            nc.vector.wait_ge(g_rs_ready, g + 1)
            for tt in range(GT):
                nc.vector.tensor_scalar(g_xn[:, tt, :], xs_tiles[:, ds(GT * g + tt, 1), :].rearrange("p a n -> p (a n)"),
                                        g_mv[:, tt, 0:1], g_rs[:, tt:tt + 1], ALU.subtract, ALU.mult).then_inc(g_xn_ready, 1)
        neg_half = sb(keep, "neg_half", [P, 8])

        att = ExitStack()
        with att:
            wq = sb(att, "wq", [P, 2, DB, D], f16)
            wo = sb(att, "wo", [P, 2, DB, D], f16)
            kd = sb(att, "kd", [P, 2, 2, HS], f16)
            vd = sb(att, "vd", [P, 2, 2, NJ, 3 * VW], f16)
            esc = sb(att, "esc", [P, 1])
            osc = sb(att, "osc", [P, 1])

            tmp = ExitStack()
            with tmp:
                wraw = [sb(tmp, f"wraw{k}", [P, DB, D]) for k in range(4)]
                wq_r, wo_r, wk_r, wv_r = wraw
                cx = sb(tmp, "cx", [P, DB, 2 * S])
                cx_rep = xs[:, 4:NP].rearrange("p i s d -> p (i s d)")[:, 0:2 * DB * HS].rearrange(
                    "p (b k n) -> p b k n", b=2, k=DB)
                kn = sb(tmp, "kn", [P, DB, 2, S])
                vr = sb(tmp, "vr", [P, 2, NJ, 3 * HD])
                vn = sb(tmp, "vn", [P, 2, NJ, 3 * VW])
                mask = sb(tmp, "mask", [P, NJ, 3 * VW])
                gate = sb(tmp, "gate", [P, 2])
                mx = sb(tmp, "mx", [P, 8])
                sc = sb(tmp, "sc", [P, 8])
                guard = sb(tmp, "guard", [P, 8])
                wf = wt[:].rearrange("p k n -> p (k n)").bitcast(f32).rearrange("p (k a n) -> p k a n", k=4, a=2)
                asum = sb(tmp, "asum", [P, 2, 4])
                asum2 = sb(tmp, "asum2", [P, 2])
                prod = sb(tmp, "prod", [P, 4])
                k_ps = bank(tmp, "k_ps", 2)
                v_ps = [bank(tmp, f"v_ps{k}") for k in range(4)]
                g_ps = bank(tmp, "g_ps")

                s_wq, s_wo, s_wk, s_wv, s_cx, s_small, s_x0, s_x1 = (sem(n) for n in (
                    "wq_loaded", "wo_loaded", "wk_loaded", "wv_loaded", "ctx_loaded", "small_loaded", "x0_loaded", "x1_loaded"))
                s_wf = [sem(f"wf_loaded{k}") for k in range(4)]
                (abs_done, pool_seq, consts, max_w, max_k, max_v, big_w, big_k, big_v, v_prod, v_out, k_prod, g_prod, rep_done,
                 dseq, kseq, vseq, sc_w, vr_zero, w_hi, kn_done, kd_hi, kd_lo, vn_done, v_hi, th_done) = (sem("s_" + n) for n in (
                    "abs_done", "pool_seq", "consts_made", "max_w", "max_k", "max_v", "big_w", "big_k", "big_v", "v_product",
                    "v_out", "k_product", "gamma_product", "ctx_replicated", "dve_seq", "k_seq", "v_seq", "w_scales", "vr_zeroed",
                    "w_hi", "k_scaled", "kd_hi", "kd_lo", "v_scaled", "v_hi", "tanh_made"))

                def kd_grid(part, q, b):
                    return kd[HD * q:HD * (q + 1), part, b, :].rearrange("p (t q s) -> p t q s", t=DB, q=HPB)[:, :, q, :]

                with nc.Block() as block:
                    @block.sync
                    def _(sp):
                        sp.dma_start(cx[:], ctx_t.rearrange(blocks, p=P)).then_inc(s_cx, 16)
                        sp.dma_start(wv_r[:], wv_t.rearrange(blocks, p=P)).then_inc(s_wv, 16)
                        sp.dma_start(wk_r[:], wk_t.rearrange(blocks, p=P)).then_inc(s_wk, 16)
                        sp.dma_start(wq_r[:], wq_t.rearrange(blocks, p=P)).then_inc(s_wq, 16)
                        sp.dma_start(xs[:, 0], x_v[:, 0]).then_inc(s_x0, 16)
                        sp.dma_start(wo_r[:], wo_t.rearrange(blocks, p=P)).then_inc(s_wo, 16)
                        sp.dma_start(lnw_s[:], lnw).then_inc(s_small, 16)
                        sp.dma_start(lnb_s[:], lnb).then_inc(s_small, 16)
                        sp.dma_start(gate[:], gates).then_inc(s_small, 16)
                        for c in range(8):
                            if c >= 4:
                                sp.wait_ge(abs_done, c - 3)
                            sp.dma_start(wf[:, c % 4], w_ffn[2 * c:2 * c + 2].rearrange("c p n -> p c n")).then_inc(s_wf[c % 4], 16)
                            if c == 1:
                                sp.dma_start(xs[:, 1], x_v[:, 1]).then_inc(s_x1, 16)
                        sp.wait_ge(s_x1, 16)

                    @block.gpsimd
                    def _(pool):
                        g = nc.gpsimd
                        g.memset(vr[:], 0.0).then_inc(vr_zero, 1)
                        g.memset(ident[:], 0.0)
                        g.memset(ones[:], 1.0)
                        g.memset(neg_half[:], -0.5)
                        g.memset(mask[:], 1.0).then_inc(pool_seq, 1)
                        pool.wait_ge(pool_seq, 1)
                        g.affine_select(out=ident[:], in_=ident[:], compare_op=ALU.not_equal, fill=1.0, base=0,
                                        pattern=[[-1, P]], channel_multiplier=1).then_inc(consts, 1)
                        for j in range(NJ):
                            h0, _ = heads_of(j)
                            m = mask[:, j, :].rearrange("p (s c) -> p s c", s=3)
                            g.affine_select(out=m, in_=m, compare_op=ALU.is_ge, fill=0.0, base=P * j - S * h0,
                                            pattern=[[-S, 3], [0, VW]], channel_multiplier=1).then_inc(pool_seq, 1)
                            pool.wait_ge(pool_seq, 2 + 2 * j)
                            last = g.affine_select(out=m, in_=m, compare_op=ALU.is_ge, fill=0.0, base=S * (h0 + 1) - 1 - P * j,
                                                   pattern=[[S, 3], [0, VW]], channel_multiplier=-1)
                            last.then_inc(pool_seq, 1)
                        g.memset(kd[:, 0], 0.0)
                        g.memset(kd[:, 1], 0.0).then_inc(pool_seq, 1)
                        pool.wait_ge(pool_seq, 2 + 2 * NJ)
                        g.memset(pool_pad[:], 0.0).then_inc(consts, 1)
                        pool.wait_ge(max_w, 3)
                        g.partition_all_reduce(big[:, 0:3], mx[:, 0:3], P, bass.bass_isa.ReduceOp.absmax).then_inc(big_w, 1)
                        pool.wait_ge(ve_ready, 1)
                        g.tensor_tensor(rs[:], ve[:], neg_half[:, 0:2], ALU.pow).then_inc(rs_ready, 1)
                        pool.wait_ge(max_k, 1)
                        g.partition_all_reduce(big[:, 3:4], mx[:, 3:4], P, bass.bass_isa.ReduceOp.absmax).then_inc(big_k, 1)
                        pool.wait_ge(kn_done, 1)
                        for q in range(HPB):
                            for b in range(2):
                                g.tensor_copy(kd_grid(0, q, b), kn[HD * q:HD * (q + 1), :, b, :]).then_inc(kd_hi, 1)
                        pool.wait_ge(kd_hi, 2 * HPB)
                        for q in range(HPB):
                            for b in range(2):
                                g.tensor_tensor(kd_grid(1, q, b), kn[HD * q:HD * (q + 1), :, b, :], kd_grid(0, q, b),
                                                ALU.subtract).then_inc(kd_lo, 1)
                        pool.wait_ge(kd_lo, 2 * HPB)
                        pool.wait_ge(max_v, 1)
                        g.partition_all_reduce(big[:, 4:5], mx[:, 4:5], P, bass.bass_isa.ReduceOp.absmax).then_inc(big_v, 1)

                    @block.tensor
                    def _(pe):
                        def v_blocks(b):
                            pe.wait_ge(rep_done, 4 * (b + 1))
                            for j in range(NJ):
                                n = b * NJ + j
                                if n >= 4:
                                    pe.wait_ge(v_out, n - 3)
                                h0, h1 = heads_of(j)
                                for k in range(DB):
                                    last = nc.tensor.matmul(v_ps[n % 4][0:rows_of(j), 0:(h1 - h0 + 1) * HD],
                                                            cx_rep[:, b, k, P * j:P * j + rows_of(j)],
                                                            wv_r[:, k, h0 * HD:(h1 + 1) * HD],
                                                            start=(k == 0), stop=(k == DB - 1))
                                last.then_inc(v_prod, 1)

                        pe.wait_ge(s_wv, 16)
                        v_blocks(0)
                        pe.wait_ge(s_cx, 16)
                        pe.wait_ge(s_wk, 16)
                        for t in range(DB):
                            for k in range(DB):
                                last = nc.tensor.matmul(k_ps[:, (t // 2) * 512 + (t % 2) * 2 * S:][:, 0:2 * S],
                                                        wk_r[:, k, t * P:(t + 1) * P], cx[:, k, :],
                                                        start=(k == 0), stop=(k == DB - 1))
                        last.then_inc(k_prod, 1)
                        v_blocks(1)
                        pe.wait_ge(consts, 1)
                        pe.wait_ge(vseq, 1)
                        nc.tensor.matmul(g_ps[:, 0:2], ones[:], asum2[:], start=True, stop=True).then_inc(g_prod, 1)

                    @block.scalar
                    def _(act):
                        a = nc.scalar

                        def v_copy(n):
                            b, j = divmod(n, NJ)
                            h0, h1 = heads_of(j)
                            act.wait_ge(v_prod, n + 1)
                            if n == 0:
                                act.wait_ge(vr_zero, 1)
                            a.copy(vr[0:rows_of(j), b, j, 0:(h1 - h0 + 1) * HD],
                                   v_ps[n % 4][0:rows_of(j), 0:(h1 - h0 + 1) * HD]).then_inc(v_out, 1)

                        def abs_sum(c):
                            act.wait_ge(s_wf[c % 4], 16 * (c // 4 + 1))
                            a.activation(wf[:, c % 4], wf[:, c % 4], ACT.Abs,
                                         accum_out=asum[:, c // 4, c % 4:c % 4 + 1]).then_inc(abs_done, 1)

                        for n in range(NJ):
                            v_copy(n)
                        act.wait_ge(s_small, 48)
                        a.activation(th[:], gate[:], ACT.Tanh).then_inc(th_done, 1)
                        for n in range(NJ, 2 * NJ):
                            v_copy(n)
                            if n in (NJ + 1, NJ + 3, NJ + 5, NJ + 7):
                                abs_sum((n - NJ) // 2)
                        act.wait_ge(sc_w, 1)
                        a.activation(wq[:, 0], wq_r[:], ACT.Copy, scale=sc[:, 0:1]).then_inc(w_hi, 1)
                        a.activation(wo[:, 0], wo_r[:], ACT.Copy, scale=sc[:, 1:2]).then_inc(w_hi, 1)
                        for c in range(4, 7):
                            abs_sum(c)
                        act.wait_ge(vn_done, 1)
                        a.copy(vd[:, 0], vn[:]).then_inc(v_hi, 1)
                        abs_sum(7)

                    @block.vector
                    def _(dve):
                        v = nc.vector
                        v.memset(sc[:], 0.0)
                        dve.wait_ge(s_cx, 16)
                        for b in range(2):
                            for k in range(DB):
                                v.tensor_copy(cx_rep[:, b, k, :].rearrange("p (h s) -> p h s", h=NH),
                                              cx[:, k, b * S:(b + 1) * S].unsqueeze(1).broadcast_to([P, NH, S])).then_inc(rep_done, 1)
                        dve.wait_ge(s_wq, 16)
                        v.tensor_reduce(mx[:, 0:1], wq_r[:].rearrange("p k n -> p (k n)"), AX.X, ALU.max,
                                        apply_absolute_value=True).then_inc(max_w, 1)
                        dve.wait_ge(s_x0, 16)
                        norm_x(0)
                        dve.wait_ge(s_wo, 16)
                        v.tensor_reduce(mx[:, 1:2], wo_r[:].rearrange("p k n -> p (k n)"), AX.X, ALU.max,
                                        apply_absolute_value=True).then_inc(max_w, 1)
                        dve.wait_ge(s_small, 48)
                        v.tensor_reduce(mx[:, 2:3], lnw_s[:], AX.X, ALU.max, apply_absolute_value=True).then_inc(max_w, 1)
                        dve.wait_ge(k_prod, 1)
                        v.tensor_copy(kn[:].rearrange("p (a t) b s -> p a (t b s)", a=2),
                                      k_ps[:, :].rearrange("p (a n) -> p a n", a=2)[:, :, 0:4 * S]).then_inc(kseq, 1)
                        dve.wait_ge(kseq, 1)
                        v.tensor_reduce(mx[:, 3:4], kn[:].rearrange("p t b s -> p (t b s)"), AX.X, ALU.max,
                                        apply_absolute_value=True).then_inc(max_k, 1)
                        dve.wait_ge(big_w, 1)
                        v.tensor_scalar(guard[:, 0:3], big[:, 0:3], 1e-30, None, ALU.max).then_inc(dseq, 1)
                        dve.wait_ge(dseq, 1)
                        v.reciprocal(inv[:, 0:3], guard[:, 0:3]).then_inc(dseq, 1)
                        dve.wait_ge(dseq, 2)
                        v.tensor_scalar(sc[:, 0:2], inv[:, 0:2], W_SCALE, None, ALU.mult).then_inc(sc_w, 1)
                        scale_x(0)
                        dve.wait_ge(big_k, 1)
                        v.tensor_scalar(guard[:, 3:4], big[:, 3:4], 1e-30, None, ALU.max).then_inc(kseq, 1)
                        dve.wait_ge(kseq, 2)
                        v.reciprocal(inv[:, 3:4], guard[:, 3:4]).then_inc(kseq, 1)
                        dve.wait_ge(kseq, 3)
                        v.tensor_scalar(kn[:], kn[:], inv[:, 3:4], W_SCALE, ALU.mult, ALU.mult).then_inc(kn_done, 1)
                        dve.wait_ge(consts, 2)
                        for b in range(2):
                            ones_of = lambda t: t.rearrange("p j (s c) -> p (j s) c", c=VW)[:, :, HD:VW]
                            v.tensor_scalar(ones_of(vn[:, b]), ones_of(mask[:]), W_SCALE, None, ALU.mult)
                        def w_low(n, w, raw):
                            dve.wait_ge(w_hi, n + 1)
                            v.scalar_tensor_tensor(w[:, 1].rearrange("p k n -> p (k n)"), raw[:].rearrange("p k n -> p (k n)"),
                                                   sc[:, n:n + 1], w[:, 0].rearrange("p k n -> p (k n)"), ALU.mult, ALU.subtract)

                        dve.wait_ge(v_out, 2 * NJ)
                        v.tensor_reduce(mx[:, 4:5], vr[:].rearrange("p b j c -> p (b j c)"), AX.X, ALU.max,
                                        apply_absolute_value=True).then_inc(max_v, 1)
                        w_low(0, wq, wq_r)
                        dve.wait_ge(big_v, 1)
                        v.tensor_scalar(guard[:, 4:5], big[:, 4:5], 1e-30, None, ALU.max).then_inc(dseq, 1)
                        dve.wait_ge(dseq, 3)
                        v.reciprocal(inv[:, 4:5], guard[:, 4:5]).then_inc(dseq, 1)
                        dve.wait_ge(dseq, 4)
                        v.tensor_scalar(sc[:, 4:5], inv[:, 4:5], W_SCALE, None, ALU.mult).then_inc(dseq, 1)
                        dve.wait_ge(dseq, 5)
                        for b in range(2):
                            values = lambda t, w: t.rearrange("p j (s c) -> p (j s) c", c=w)[:, :, 0:HD]
                            last = v.scalar_tensor_tensor(values(vn[:, b], VW), values(vr[:, b], HD), sc[:, 4:5],
                                                          values(mask[:], VW), ALU.mult, ALU.mult)
                        last.then_inc(vn_done, 1)
                        w_low(1, wo, wo_r)
                        dve.wait_ge(th_done, 1)
                        v.tensor_tensor(prod[:, 0:1], big[:, 0:1], big[:, 3:4], ALU.mult)
                        v.tensor_tensor(prod[:, 1:2], big[:, 1:2], big[:, 4:5], ALU.mult).then_inc(dseq, 1)
                        dve.wait_ge(dseq, 6)
                        v.tensor_scalar(esc[:], prod[:, 0:1], HD ** -0.5 / (X_SCALE * W_SCALE * Q_SHIFT * W_SCALE), None, ALU.mult)
                        v.tensor_scalar(osc[:], prod[:, 1:2], th[:, 0:1], 1.0 / (W_SCALE * W_SCALE), ALU.mult, ALU.mult)
                        dve.wait_ge(v_hi, 1)
                        v.tensor_tensor(vd[:, 1].rearrange("p b j c -> p (b j c)"), vn[:].rearrange("p b j c -> p (b j c)"),
                                        vd[:, 0].rearrange("p b j c -> p (b j c)"), ALU.subtract)
                        dve.wait_ge(abs_done, 8)
                        v.tensor_reduce(asum2[:], asum[:], AX.X, ALU.add).then_inc(vseq, 1)
                        dve.wait_ge(g_prod, 1)
                        v.tensor_scalar(thr[:, 0, :], g_ps[:, 0:2], 1.0 / (HF * D), GAMMA_EPS, ALU.mult, ALU.add).then_inc(vseq, 1)
                        dve.wait_ge(vseq, 2)
                        v.tensor_scalar(thr[:, 1, :], thr[:, 0, :], -0.5, None, ALU.mult).then_inc(vseq, 1)
                        dve.wait_ge(vseq, 3)
                        v.tensor_scalar(thr[:, 0, :], thr[:, 1, :], -1.0, None, ALU.mult).then_inc(vseq, 1)
                        dve.wait_ge(vseq, 4)
                        for w in range(2):
                            v.tensor_copy(thr_c[:, 8 * w:8 * w + 8, :], thr[:, :, w].unsqueeze(1).broadcast_to([P, 8, 2]))

            run = ExitStack()
            with run:
                xt = sb(run, "xt", [P, 2, DB, 2 * P], f16)
                q = sb(run, "q", [P, 2, DB, 2 * P], f16)
                pr = sb(run, "pr", [P, 2, NJ * P])
                mxs = sb(run, "mxs", [P, 2, NH])
                pt = sb(run, "pt", [P, 2, 2, NJ * P], f16)
                rc = sb(run, "rc", [P, 2, NH])
                o = sb(run, "o", [P, 2, D])
                ot = sb(run, "ot", [P, 2, 2, DB, P], f16)
                wc = sb(run, "wc", [P, CW])
                wa = sb(run, "wa", [P, CW])
                wb = sb(run, "wb", [P, CW])
                tc = sb(run, "tc", [P, 2])
                sc_ps = bank(run, "sc_ps", 3)
                five = bank(run, "five", 5)
                V1, T0, T1, X0, V0 = (five[:, 512 * n:512 * (n + 1)] for n in range(5))
                PT_BANKS = ((T0, T1, X0), (T1, X0, V0))
                PT_BLOCKS = ((0, 4), (4, 8), (8, NJ))
                PV_BANKS = ((V1, T0), (X0, V0))
                PV_BOTH = [five[:, 512 * n:512 * (n + 2)].rearrange("p (a c) -> p a c", a=2)[:, :, 0:8 * VW].rearrange(
                    "p a (h c) -> p a h c", h=8) for n in (0, 3)]
                Q_BANKS = (V1, V0)
                XT_BANKS = (V1, T1)
                OT_BANKS = (T0, X0)
                O_BANKS = (T0, V0)

                (x_in, xt_prod, xt_hi, xt_ready, q_prod, q_hi, q_ready, sc_prod, maxd, shifted,
                 expd, pt_prod, pt_hi, pt_ready, pv_prod, rcp, normed, ot_prod, ot_hi, ot_ready, o_prod, x_done,
                 w_in, w_cmp, w_done, t_cur, pr_zero) = (sem("a_" + n) for n in (
                    "x_in", "xt_product", "xt_hi", "xt_ready", "q_product", "q_hi",
                    "q_ready", "scores_product", "maxima", "scores_shifted", "exp_done", "pt_product", "pt_hi", "pt_ready",
                    "pv_product", "rcp_done", "o_normed", "ot_product", "ot_hi", "ot_ready", "o_product", "x_done",
                    "w_in", "w_compared", "w_done", "threshold_set", "pr_zeroed"))


                with nc.Block() as block:
                    @block.sync
                    def _(sp):
                        sp.dma_start(wc[:], w_ffn[0]).then_inc(w_in, 16)

                        def load_x(i):
                            sp.dma_start(xs[:, ds(i, 1)], x_v[:, ds(i, 1)]).then_inc(x_in, 16)

                        def load_chunk(i):
                            sp.wait_ge(w_done, i)
                            sp.dma_start(wc[:], w_ffn[ds(i, 1)].rearrange("c p n -> p (c n)")).then_inc(w_in, 16)

                        load_x(2)
                        sp.wait_ge(x_in, 16)
                        load_x(3)
                        with sp.Fori(1, NP - 3) as i:
                            sp.wait_ge(x_in, 16 * i + 16)
                            load_x(i + 3)
                            load_chunk(i)
                        for i in range(NP - 3, NP):
                            load_chunk(i)

                    @block.gpsimd
                    def _(pool):
                        g = nc.gpsimd

                        def carry_wait():
                            g.tensor_tensor(pool_pad[:], neg_half[:, 0:1], neg_half[:, 1:2], ALU.mult)

                        def rstd(i):
                            pool.wait_ge(ve_ready, i + 1)
                            g.tensor_tensor(rs[:], ve[:], neg_half[:, 0:2], ALU.pow).then_inc(rs_ready, 1)

                        def ternarize(i):
                            pool.wait_ge(w_in, 16 * i + 16)
                            carry_wait()
                            g.tensor_copy(tc[:], thr_c[:, ds(i, 1), :].rearrange("p a b -> p (a b)")).then_inc(t_cur, 1)
                            pool.wait_ge(t_cur, i + 1)
                            carry_wait()
                            g.tensor_scalar(wa[:], wc[:], tc[:, 0:1], None, ALU.is_gt)
                            g.tensor_scalar(wb[:], wc[:], tc[:, 1:2], None, ALU.is_lt).then_inc(w_cmp, 1)
                            pool.wait_ge(w_cmp, i + 1)
                            g.tensor_tensor(wt[:, ds(i, 1), :].rearrange("p a n -> p (a n)"), wa[:], wb[:],
                                            ALU.subtract).then_inc(w_done, 1)

                        rstd(1)
                        rstd(2)
                        with pool.Fori(0, NP - 3) as i:
                            rstd(i + 3)
                            ternarize(i)
                        ternarize(NP - 3)
                        pool.wait_ge(g_ve_ready, 1)
                        g.tensor_tensor(g_rs[:], g_ve[:], neg_half[:, 0:GT], ALU.pow).then_inc(g_rs_ready, 1)
                        ternarize(NP - 2)
                        ternarize(NP - 1)

                    @block.tensor
                    def _(pe):
                        mm = nc.tensor.matmul

                        def transpose_x(i, s):
                            pe.wait_ge(xn_ready, 2 * i + s + 1)
                            for k in range(DB):
                                last = nc.tensor.transpose(XT_BANKS[s][:, k * P:(k + 1) * P], xn[:, s, k * P:(k + 1) * P], ident[:])
                            last.then_inc(xt_prod, 1)

                        def project_q(i, half, blocks=(0, 1)):
                            pe.wait_ge(xt_ready, 2 * i + 2)
                            for t in (2 * half + k for k in blocks):
                                for n, (a, b) in enumerate(QKV_ORDER):
                                    for k in range(DB):
                                        last = mm(Q_BANKS[half][:, (t % 2) * 2 * P:(t % 2 + 1) * 2 * P],
                                                  wq[:, a, k, t * P:(t + 1) * P], xt[:, b, k, :],
                                                  start=(n == 0 and k == 0), stop=(n == 2 and k == DB - 1))
                            if 1 in blocks:
                                last.then_inc(q_prod, 1)

                        def scores(i, s):
                            pe.wait_ge(q_ready, 2 * i + 2)
                            for t in range(DB):
                                c0, c1 = t * HPB * S, (t + 1) * HPB * S
                                cut = [c0] + [c for c in (512, 1024) if c0 < c < c1] + [c1]
                                for lo, hi in zip(cut, cut[1:]):
                                    for n, (a, b) in enumerate(QKV_ORDER):
                                        last = mm(sc_ps[:, lo:hi], q[:, a, t, s * P:(s + 1) * P], kd[:, b, s, lo:hi],
                                                  start=(n == 0), stop=(n == 2))
                            last.then_inc(sc_prod, 1)

                        def transpose_p(i, s, final):
                            pe.wait_ge(expd, 2 * i + s + 1)
                            for c, (j0, j1) in enumerate(PT_BLOCKS):
                                if s == 1 and c == 2 and not final:
                                    pe.wait_ge(q_ready, 2 * i + 4)
                                for j in range(j0, j1):
                                    last = nc.tensor.transpose(PT_BANKS[s][c][:, (j - j0) * P:(j - j0 + 1) * P],
                                                               pr[:, s, P * j:P * (j + 1)], ident[:])
                                last.then_inc(pt_prod, 1)

                        def weigh_v(i, s):
                            pe.wait_ge(pt_ready, 3 * (2 * i + s) + 3)
                            first = [True, True]
                            for j in range(NJ):
                                h0, h1 = heads_of(j)
                                parts = [(h0, min(h1, 7), 0)] if h0 < 8 else []
                                parts += [(max(h0, 8), h1, 1)] if h1 >= 8 else []
                                for ha, hb, side in parts:
                                    for n, (a, b) in enumerate(QKV_ORDER):
                                        final = n == 2 and (hb == 7 and j == 4 or j == NJ - 1)
                                        last = mm(PV_BANKS[s][side][:, (ha % 8) * VW:(hb % 8 + 1) * VW],
                                                  pt[:, s, a, P * j:P * (j + 1)],
                                                  vd[:, b, s, j, (ha - h0) * VW:(hb - h0 + 1) * VW],
                                                  start=first[side], stop=final, skip_group_check=True)
                                        first[side] = False
                            last.then_inc(pv_prod, 1)

                        def transpose_o(i, s):
                            pe.wait_ge(normed, 2 * i + s + 1)
                            for k in range(DB):
                                last = nc.tensor.transpose(OT_BANKS[s][:, k * P:(k + 1) * P], o[:, s, k * P:(k + 1) * P], ident[:])
                            last.then_inc(ot_prod, 1)

                        def project_o(i, s):
                            pe.wait_ge(ot_ready, 2 * i + s + 1)
                            for n, (a, b) in enumerate(QKV_ORDER):
                                for k in range(DB):
                                    last = mm(O_BANKS[s][:, :], ot[:, s, a, k, :], wo[:, b, k, :],
                                              start=(n == 0 and k == 0), stop=(n == 2 and k == DB - 1))
                            last.then_inc(o_prod, 1)

                        def transpose_group(tt, to):
                            pe.wait_ge(g_xn_ready, tt + 1)
                            for k in range(DB):
                                last = nc.tensor.transpose(to[:, k * P:(k + 1) * P], g_xn[:, tt, k * P:(k + 1) * P], ident[:])
                            last.then_inc(g_xt_prod, 1)

                        def one_pair(i, first=False, q_ahead=True, x_ahead=True):
                            if not first:
                                pe.wait_ge(shifted, 2 * i)
                            scores(i, 0)
                            if not first:
                                project_o(i - 1, 1)
                            if q_ahead:
                                project_q(i + 1, 0, (0,))
                            else:
                                transpose_group(0, V1)
                            pe.wait_ge(shifted, 2 * i + 1)
                            scores(i, 1)
                            if q_ahead:
                                project_q(i + 1, 0, (1,))
                            if not first:
                                pe.wait_ge(x_done, 2 * i - 1)
                            transpose_p(i, 0, not q_ahead)
                            if not first:
                                pe.wait_ge(x_done, 2 * i)
                            if q_ahead:
                                project_q(i + 1, 1)
                                pe.wait_ge(q_ready, 2 * i + 3)
                            else:
                                transpose_group(1, V0)
                                pe.wait_ge(g_xt_ready, 2)
                            weigh_v(i, 0)
                            transpose_p(i, 1, not q_ahead)
                            transpose_o(i, 0)
                            if x_ahead or not q_ahead:
                                if x_ahead:
                                    transpose_x(i + 2, 0)
                                else:
                                    transpose_group(2, V1)
                                pe.wait_ge(pt_ready, 3 * (2 * i + 1) + 1)
                                if x_ahead:
                                    transpose_x(i + 2, 1)
                                else:
                                    transpose_group(3, T1)
                            weigh_v(i, 1)
                            project_o(i, 0)
                            transpose_o(i, 1)

                        pe.wait_ge(pr_zero, 1)
                        transpose_x(0, 0)
                        transpose_x(0, 1)
                        project_q(0, 0)
                        project_q(0, 1)
                        pe.wait_ge(q_ready, 1)
                        transpose_x(1, 0)
                        transpose_x(1, 1)
                        one_pair(0, first=True)
                        with pe.Fori(1, NP - 2) as i:
                            one_pair(i)
                        one_pair(NP - 2, x_ahead=False)
                        one_pair(NP - 1, q_ahead=False, x_ahead=False)
                        project_o(NP - 1, 1)

                    @block.scalar
                    def _(act):
                        a = nc.scalar

                        def x_high(i, s):
                            act.wait_ge(xt_prod, 2 * i + s + 1)
                            a.copy(xt[:, 0, :, s * P:(s + 1) * P],
                                   XT_BANKS[s][:, :].rearrange("p (k n) -> p k n", k=DB)).then_inc(xt_hi, 1)

                        def q_high(i, half):
                            act.wait_ge(q_prod, 2 * i + half + 1)
                            a.mul(q[:, 0, 2 * half:2 * half + 2, :],
                                  Q_BANKS[half][:, :].rearrange("p (t n) -> p t n", t=2), Q_SHIFT).then_inc(q_hi, 1)

                        def exp(i, s):
                            act.wait_ge(shifted, 2 * i + s + 1)
                            a.activation(pr[:, s, 0:HS], pr[:, s, 0:HS], ACT.Exp, scale=esc[:]).then_inc(expd, 1)

                        def p_high(i, s):
                            for c, (j0, j1) in enumerate(PT_BLOCKS):
                                act.wait_ge(pt_prod, 3 * (2 * i + s) + c + 1)
                                a.mul(pt[:, s, 0, P * j0:P * j1], PT_BANKS[s][c][:, 0:P * (j1 - j0)], P_SCALE).then_inc(pt_hi, 1)

                        def o_high(i, s):
                            act.wait_ge(ot_prod, 2 * i + s + 1)
                            a.mul(ot[:, s, 0].rearrange("p k n -> p (k n)"), OT_BANKS[s][:, :], W_SCALE).then_inc(ot_hi, 1)

                        def group_high(tt, bank_):
                            act.wait_ge(g_xt_prod, tt + 1)
                            a.copy(g_xt[:, 0, :, tt * P:(tt + 1) * P], bank_.rearrange("p (k n) -> p k n", k=DB)).then_inc(g_xt_hi, 1)

                        def one_pair(i, q_ahead=True, x_ahead=True):
                            if not q_ahead:
                                group_high(0, V1)
                            exp(i, 0)
                            if q_ahead:
                                q_high(i + 1, 0)
                            p_high(i, 0)
                            if not q_ahead:
                                group_high(1, V0)
                            exp(i, 1)
                            if q_ahead:
                                q_high(i + 1, 1)
                            p_high(i, 1)
                            o_high(i, 0)
                            if x_ahead:
                                x_high(i + 2, 0)
                                x_high(i + 2, 1)
                            if not q_ahead:
                                group_high(2, V1)
                                group_high(3, T1)
                            o_high(i, 1)

                        x_high(0, 0)
                        x_high(0, 1)
                        q_high(0, 0)
                        q_high(0, 1)
                        x_high(1, 0)
                        x_high(1, 1)
                        with act.Fori(0, NP - 2) as i:
                            one_pair(i)
                        one_pair(NP - 2, x_ahead=False)
                        one_pair(NP - 1, q_ahead=False, x_ahead=False)

                    @block.vector
                    def _(dve):
                        v = nc.vector

                        def x_low(i, s):
                            dve.wait_ge(xt_hi, 2 * i + s + 1)
                            v.tensor_tensor(xt[:, 1, :, s * P:(s + 1) * P],
                                            XT_BANKS[s][:, :].rearrange("p (k n) -> p k n", k=DB),
                                            xt[:, 0, :, s * P:(s + 1) * P], ALU.subtract).then_inc(xt_ready, 1)

                        def q_low(i, half):
                            dve.wait_ge(q_hi, 2 * i + half + 1)
                            v.scalar_tensor_tensor(q[:, 1, 2 * half:2 * half + 2, :].rearrange("p t n -> p (t n)"),
                                                   Q_BANKS[half][:, :], Q_SHIFT,
                                                   q[:, 0, 2 * half:2 * half + 2, :].rearrange("p t n -> p (t n)"),
                                                   ALU.mult, ALU.subtract).then_inc(q_ready, 1)

                        def shift_scores(i, s):
                            dve.wait_ge(sc_prod, 2 * i + s + 1)
                            grid = sc_ps[:, 0:HS].rearrange("p (h k) -> p h k", h=NH)
                            v.tensor_reduce(mxs[:, s, :], grid, AX.X, ALU.max).then_inc(maxd, 1)
                            dve.wait_ge(maxd, 2 * i + s + 1)
                            v.tensor_tensor(pr[:, s, 0:HS].rearrange("p (h k) -> p h k", h=NH), grid,
                                            mxs[:, s, :].unsqueeze(2).broadcast_to([P, NH, S]), ALU.subtract).then_inc(shifted, 1)

                        def p_low(i, s):
                            for c, (j0, j1) in enumerate(PT_BLOCKS):
                                dve.wait_ge(pt_hi, 3 * (2 * i + s) + c + 1)
                                v.scalar_tensor_tensor(pt[:, s, 1, P * j0:P * j1], PT_BANKS[s][c][:, 0:P * (j1 - j0)], P_SCALE,
                                                       pt[:, s, 0, P * j0:P * j1], ALU.mult, ALU.subtract).then_inc(pt_ready, 1)

                        def norm_o(i, s):
                            dve.wait_ge(pv_prod, 2 * i + s + 1)
                            sums, values = PV_BOTH[s][:, :, :, HD], PV_BOTH[s][:, :, :, 0:HD]
                            v.reciprocal(rc[:, s, :].rearrange("p (a h) -> p a h", a=2), sums).then_inc(rcp, 1)
                            dve.wait_ge(rcp, 2 * i + s + 1)
                            v.tensor_tensor(o[:, s, :].rearrange("p (a h c) -> p a h c", a=2, h=8), values,
                                            rc[:, s, :].rearrange("p (a h) -> p a h", a=2).unsqueeze(3).broadcast_to([P, 2, 8, HD]),
                                            ALU.mult).then_inc(normed, 1)

                        def o_low(i, s):
                            dve.wait_ge(ot_hi, 2 * i + s + 1)
                            v.scalar_tensor_tensor(ot[:, s, 1].rearrange("p k n -> p (k n)"), OT_BANKS[s][:, :], W_SCALE,
                                                   ot[:, s, 0].rearrange("p k n -> p (k n)"),
                                                   ALU.mult, ALU.subtract).then_inc(ot_ready, 1)

                        def add_branch(i, s):
                            dve.wait_ge(o_prod, 2 * i + s + 1)
                            tile = xs[:, ds(i, 1), s, :].rearrange("p a n -> p (a n)")
                            v.scalar_tensor_tensor(tile, O_BANKS[s][:, :], osc[:], tile, ALU.mult, ALU.add).then_inc(x_done, 1)

                        def group_low(tt, bank_):
                            dve.wait_ge(g_xt_hi, tt + 1)
                            v.tensor_tensor(g_xt[:, 1, :, tt * P:(tt + 1) * P], bank_.rearrange("p (k n) -> p k n", k=DB),
                                            g_xt[:, 0, :, tt * P:(tt + 1) * P], ALU.subtract).then_inc(g_xt_ready, 1)

                        def one_pair(i, first=False, q_ahead=True, x_ahead=True, norm_ahead=True):
                            shift_scores(i, 0)
                            if not first:
                                add_branch(i - 1, 1)
                            if norm_ahead:
                                dve.wait_ge(x_in, 16 * i + 32)
                                norm_x(i + 3)
                            if not q_ahead:
                                group_low(0, V1)
                            shift_scores(i, 1)
                            if q_ahead:
                                q_low(i + 1, 0)
                            p_low(i, 0)
                            if q_ahead:
                                q_low(i + 1, 1)
                            else:
                                group_low(1, V0)
                            norm_o(i, 0)
                            p_low(i, 1)
                            o_low(i, 0)
                            if x_ahead:
                                x_low(i + 2, 0)
                                x_low(i + 2, 1)
                            if not q_ahead:
                                group_low(2, V1)
                                group_low(3, T1)
                            norm_o(i, 1)
                            if norm_ahead:
                                scale_x(i + 3)
                            add_branch(i, 0)
                            o_low(i, 1)

                        v.memset(pr[:, :, HS:NJ * P], 0.0).then_inc(pr_zero, 1)
                        x_low(0, 0)
                        x_low(0, 1)
                        norm_x(1)
                        scale_x(1)
                        q_low(0, 0)
                        q_low(0, 1)
                        dve.wait_ge(x_in, 16)
                        norm_x(2)
                        x_low(1, 0)
                        x_low(1, 1)
                        scale_x(2)
                        one_pair(0, first=True)
                        with dve.Fori(1, NP - 3) as i:
                            one_pair(i)
                        one_pair(NP - 3, norm_ahead=False)
                        norm_group(0)
                        one_pair(NP - 2, x_ahead=False, norm_ahead=False)
                        scale_group(0)
                        one_pair(NP - 1, q_ahead=False, x_ahead=False, norm_ahead=False)
                        add_branch(NP - 1, 1)

        ffn = ExitStack()
        with ffn:
            GR = 8
            gf = sb(ffn, "gf", [P, GR, GT * P])
            sq = sb(ffn, "sq", [P, 4, GT * P])
            s12 = sb(ffn, "s12", [P, 2, GT * P])
            gw = sb(ffn, "gw", [P, 2, HB, GT * P], f16)
            zero = sb(ffn, "zero", [P, GT * P])
            wsc = sb(ffn, "wsc", [P, HB])
            parts = sb(ffn, "parts", [P, HB, 6], bf16)
            rest = sb(ffn, "rest", [P, 2, HB])
            colsum = sb(ffn, "colsum", [6, D])
            pick = sb(ffn, "pick", [6, 2, P])
            cw = sb(ffn, "cw", [P, D])
            cb = sb(ffn, "cb", [P, D])
            fsc = sb(ffn, "fsc", [P, 1])
            tot = sb(ffn, "tot", [P, 2, GT])
            negm = sb(ffn, "negm", [P, GT])
            m2 = sb(ffn, "m2", [P, GT])
            ge = sb(ffn, "ge", [P, GT])
            grs = sb(ffn, "grs", [P, GT])
            gr = sb(ffn, "gr", [P, GT])
            t1 = sb(ffn, "t1", [P, D])
            t2 = sb(ffn, "t2", [P, D])
            ob = sb(ffn, "ob", [P, 2, D])
            Z = [bank(ffn, f"Z{k}") for k in range(4)]
            R = [bank(ffn, f"R{k}") for k in range(2)]
            XB = bank(ffn, "XB")
            SB = bank(ffn, "SB")

            (pieces, picked, fseq, c6, c6_out, cwb, c_done,
             z_prod, gelu_done, sq_done, s1_done, s2_done, gw_hi, gw_ready, r_prod, st_prod, sseq, ge_ready, grs_ready,
             r_read, fin, ob_ready, sums_out) = (sem("f_" + n) for n in (
                "pieces_made", "pick_made", "dve_seq", "column_sums", "column_sums_out", "column_sums_bcast", "consts_done",
                "z_product", "gelu_done",
                "sq_done", "s1_done", "s2_done", "gw_hi", "gw_ready", "r_product", "stats_product", "stats_seq", "ge_ready",
                "grs_ready", "r_read", "final_seq", "ob_ready", "sums_out"))
            stored = [sem("f_stored0"), sem("f_stored1")]


            with nc.Block() as block:
                @block.sync
                def _(sp):
                    with sp.Fori(0, NG) as g:
                        for tt in range(GT):
                            sp.wait_ge(ob_ready, GT * g + tt + 1)
                            sp.dma_start(out_v[:, ds(2 * g + tt // 2, 1), tt % 2, :],
                                         ob[:, tt % 2:tt % 2 + 1, :]).then_inc(stored[tt % 2], 16)
                    for k in range(2):
                        sp.wait_ge(stored[k], 16 * NT // 2)

                @block.gpsimd
                def _(pool):
                    g_ = nc.gpsimd
                    g_.memset(zero[:], 0.0)
                    g_.memset(pick[:], 1.0).then_inc(picked, 1)
                    pool.wait_ge(picked, 1)
                    g_.affine_select(out=pick[:, 0, :], in_=pick[:, 0, :], compare_op=ALU.is_ge, fill=0.0, base=2,
                                     pattern=[[0, P]], channel_multiplier=-1)
                    g_.affine_select(out=pick[:, 1, :], in_=pick[:, 1, :], compare_op=ALU.is_ge, fill=0.0, base=-3,
                                     pattern=[[0, P]], channel_multiplier=1).then_inc(picked, 1)

                    def rstd(g):
                        pool.wait_ge(g_ve_ready, g + 1)
                        g_.tensor_tensor(g_rs[:], g_ve[:], neg_half[:, 0:GT], ALU.pow).then_inc(g_rs_ready, 1)

                    def group(g, norm_ahead=True):
                        for h in range(HB):
                            pool.wait_ge(sq_done, HB * g + h + 1)
                            if h == 0:
                                g_.tensor_tensor(s12[:, 1], sq[:, 0], zero[:], ALU.add).then_inc(s2_done, 1)
                            else:
                                pool.wait_ge(s2_done, HB * g + h)
                                g_.tensor_tensor(s12[:, 1], s12[:, 1], sq[:, h % 4], ALU.add).then_inc(s2_done, 1)
                        pool.wait_ge(ge_ready, g + 1)
                        g_.tensor_tensor(grs[:], ge[:], neg_half[:, 0:GT], ALU.pow).then_inc(grs_ready, 1)
                        if norm_ahead:
                            rstd(g + 2)

                    rstd(1)
                    with pool.Fori(0, NG - 2) as g:
                        group(g)
                    group(NG - 2, norm_ahead=False)
                    group(NG - 1, norm_ahead=False)

                @block.tensor
                def _(pe):
                    mm = nc.tensor.matmul

                    def transpose_x(g, tt, to):
                        pe.wait_ge(g_xn_ready, GT * g + tt + 1)
                        for k in range(DB):
                            last = nc.tensor.transpose(to[:, k * P:(k + 1) * P], g_xn[:, tt, k * P:(k + 1) * P], ident[:])
                        last.then_inc(g_xt_prod, 1)

                    def up(g, h, first):
                        if not (first and h < 4):
                            pe.wait_ge(gelu_done, HB * g + h - 3)
                        for k in range(DB):
                            for a in range(2):
                                last = mm(Z[h % 4][:, :], wfc[:, k, h * P:(h + 1) * P], g_xt[:, a, k, :],
                                          start=(k == 0 and a == 0), stop=(k == DB - 1 and a == 1))
                        last.then_inc(z_prod, 1)

                    def down(g, tt, first):
                        if not (first and tt < 2):
                            pe.wait_ge(r_read, GT * g + tt - 1)
                        for h in range(HB):
                            if tt == 0:
                                pe.wait_ge(gw_ready, HB * g + h + 1)
                            for a in range(2):
                                last = mm(R[tt % 2][:, :], gw[:, a, h, tt * P:(tt + 1) * P], wpr[:, h, :],
                                          start=(h == 0 and a == 0), stop=(h == HB - 1 and a == 1))
                        last.then_inc(r_prod, 1)

                    def turn_sums(g, k):
                        for tt in range(GT):
                            last = nc.tensor.transpose((SB, XB)[k][:, tt * P:(tt + 1) * P], s12[:, k, tt * P:(tt + 1) * P], ident[:])
                        last.then_inc(st_prod, 1)

                    def column_sums():
                        pe.wait_ge(pieces, 1)
                        for h in range(HB):
                            last = mm(R[0][0:6, :], parts[:, h, :], wpr[:, h, :], start=(h == 0), stop=(h == HB - 1))
                        last.then_inc(c6, 1)

                    def spread_sums():
                        pe.wait_ge(c6_out, 1)
                        pe.wait_ge(picked, 2)
                        mm(R[1][:, :], pick[:, 0, :], colsum[:], start=True, stop=True)
                        mm(SB[:, :], pick[:, 1, :], colsum[:], start=True, stop=True).then_inc(cwb, 1)

                    def group(g, first=False, final=False):
                        pe.wait_ge(g_xt_ready, GT * g + GT)
                        for h in range(HB):
                            up(g, h, first)
                            if first and h == 8:
                                column_sums()
                            if first and h == 11:
                                spread_sums()
                        if first:
                            pe.wait_ge(c_done, 1)
                        for tt in range(GT):
                            if not final:
                                if tt:
                                    pe.wait_ge(*((sums_out, 2 * g + 2) if tt == 1 else (g_xt_ready, GT * g + GT + tt)))
                                transpose_x(g + 1, tt, XB)
                            down(g, tt, first)
                            if tt == 0:
                                pe.wait_ge(s1_done, HB * g + HB)
                                turn_sums(g, 0)
                                pe.wait_ge(s2_done, HB * g + HB)
                                if not final:
                                    pe.wait_ge(g_xt_ready, GT * g + GT + 1)
                                turn_sums(g, 1)

                    group(0, first=True)
                    with pe.Fori(1, NG - 1) as g:
                        group(g)
                    group(NG - 1, final=True)

                @block.scalar
                def _(act):
                    a_ = nc.scalar

                    def x_high(g, tt, bank_):
                        act.wait_ge(g_xt_prod, GT * g + tt + 1)
                        a_.copy(g_xt[:, 0, :, tt * P:(tt + 1) * P], bank_[:, :].rearrange("p (k n) -> p k n", k=DB)).then_inc(g_xt_hi, 1)

                    def square(g, h, first):
                        act.wait_ge(gelu_done, HB * g + h + 1)
                        if not (first and h < 4):
                            act.wait_ge(s2_done, HB * g + h - 3)
                        a_.activation(sq[:, h % 4], gf[:, h % GR], ACT.Square).then_inc(sq_done, 1)

                    def gelu(g, h, first):
                        act.wait_ge(z_prod, HB * g + h + 1)
                        if not (first and h < GR):
                            act.wait_ge(s1_done, HB * g + h - GR + 1)
                        a_.activation(gf[:, h % GR], Z[h % 4][:, :], ACT.Gelu, scale=1.0 / X_SCALE).then_inc(gelu_done, 1)

                    def group(g, first=False, final=False):
                        for h in range(HB):
                            gelu(g, h, first)
                            if h:
                                square(g, h - 1, first)
                        square(g, HB - 1, first)
                        if not final:
                            for tt in range(GT):
                                x_high(g + 1, tt, XB)

                    group(0, first=True)
                    with act.Fori(1, NG - 1) as g:
                        group(g)
                    group(NG - 1, final=True)

                @block.vector
                def _(dve):
                    v = nc.vector

                    def x_low(g, tt, bank_):
                        dve.wait_ge(g_xt_hi, GT * g + tt + 1)
                        v.tensor_tensor(g_xt[:, 1, :, tt * P:(tt + 1) * P], bank_[:, :].rearrange("p (k n) -> p k n", k=DB),
                                        g_xt[:, 0, :, tt * P:(tt + 1) * P], ALU.subtract).then_inc(g_xt_ready, 1)

                    def split_g(g, h, first):
                        dve.wait_ge(gelu_done, HB * g + h + 1)
                        if h == 0 and not first:
                            dve.wait_ge(r_prod, GT * g)
                        v.tensor_scalar(gw[:, 0, h, :], gf[:, h % GR], wsc[:, h:h + 1], None, ALU.mult).then_inc(gw_hi, 1)
                        dve.wait_ge(gw_hi, HB * g + h + 1)
                        v.scalar_tensor_tensor(gw[:, 1, h, :], gf[:, h % GR], wsc[:, h:h + 1], gw[:, 0, h, :],
                                               ALU.mult, ALU.subtract).then_inc(gw_ready, 1)
                        if h == 0:
                            v.tensor_copy(s12[:, 0], gf[:, 0]).then_inc(s1_done, 1)
                        else:
                            dve.wait_ge(s1_done, HB * g + h)
                            v.tensor_tensor(s12[:, 0], s12[:, 0], gf[:, h % GR], ALU.add).then_inc(s1_done, 1)

                    def moments(g):
                        for k in range(2):
                            dve.wait_ge(st_prod, 2 * g + k + 1)
                            v.tensor_reduce(tot[:, k, :], (SB, XB)[k][:, :].rearrange("p (t n) -> p t n", t=GT), AX.X,
                                            ALU.add).then_inc(sums_out, 1)
                        dve.wait_ge(sums_out, 2 * g + 2)
                        v.tensor_scalar(negm[:], tot[:, 0, :], -1.0 / HF, None, ALU.mult).then_inc(sseq, 1)
                        dve.wait_ge(sseq, 3 * g + 1)
                        v.tensor_tensor(m2[:], negm[:], negm[:], ALU.mult).then_inc(sseq, 1)
                        dve.wait_ge(sseq, 3 * g + 2)
                        v.scalar_tensor_tensor(ge[:], tot[:, 1, :], 1.0 / HF, m2[:], ALU.mult, ALU.subtract).then_inc(sseq, 1)
                        dve.wait_ge(sseq, 3 * g + 3)
                        v.tensor_scalar(ge[:], ge[:], 0.0, LN_EPS, ALU.max, ALU.add).then_inc(ge_ready, 1)
                        dve.wait_ge(grs_ready, g + 1)
                        v.tensor_scalar(gr[:], grs[:], fsc[:], None, ALU.mult).then_inc(fin, 1)

                    def finish(g, tt, first):
                        n = GT * g + tt
                        dve.wait_ge(r_prod, n + 1)
                        if tt == 0:
                            dve.wait_ge(fin, 5 * g + 1)
                        v.scalar_tensor_tensor(t1[:], cw[:], negm[:, tt:tt + 1], R[tt % 2][:, :], ALU.mult, ALU.add).then_inc(r_read, 1)
                        dve.wait_ge(r_read, n + 1)
                        v.scalar_tensor_tensor(t2[:], t1[:], gr[:, tt:tt + 1],
                                               xs_tiles[:, ds(n, 1), :].rearrange("p a n -> p (a n)"), ALU.mult, ALU.add).then_inc(fin, 1)
                        dve.wait_ge(fin, 5 * g + tt + 2)
                        if not (first and tt < 2):
                            dve.wait_ge(stored[tt % 2], 16 * (2 * g + tt // 2))
                        v.tensor_tensor(ob[:, tt % 2, :], t2[:], cb[:], ALU.add).then_inc(ob_ready, 1)

                    def group(g, first=False, final=False, norm_ahead=True):
                        for h in range(HB):
                            split_g(g, h, first)
                            if first and h == 8:
                                dve.wait_ge(c6, 1)
                                v.tensor_copy(colsum[:], R[0][0:6, :]).then_inc(c6_out, 1)
                            if first and h == 12:
                                dve.wait_ge(cwb, 1)
                                v.tensor_copy(cw[:], R[1][:, :])
                                v.tensor_scalar(cb[:], SB[:, :], th[:, 1:2], None, ALU.mult).then_inc(c_done, 1)
                        if not final:
                            x_low(g + 1, 0, XB)
                        moments(g)
                        for tt in range(GT):
                            finish(g, tt, first)
                            if tt < GT - 1 and not final:
                                x_low(g + 1, tt + 1, XB)
                            if tt == 1 and norm_ahead:
                                norm_group(g + 2)
                        if norm_ahead:
                            scale_group(g + 2)

                    norm_group(1)
                    v.tensor_scalar(wsc[:], lnw_s[:], inv[:, 2:3], G_SCALE, ALU.mult, ALU.mult).then_inc(fseq, 1)
                    dve.wait_ge(fseq, 1)
                    v.tensor_copy(parts[:, :, 0], wsc[:])
                    v.tensor_copy(parts[:, :, 3], lnb_s[:]).then_inc(fseq, 1)
                    dve.wait_ge(fseq, 2)
                    v.tensor_tensor(rest[:, 0, :], wsc[:], parts[:, :, 0], ALU.subtract)
                    v.tensor_tensor(rest[:, 1, :], lnb_s[:], parts[:, :, 3], ALU.subtract).then_inc(fseq, 1)
                    dve.wait_ge(fseq, 3)
                    v.tensor_copy(parts[:, :, 1], rest[:, 0, :])
                    v.tensor_copy(parts[:, :, 4], rest[:, 1, :]).then_inc(fseq, 1)
                    dve.wait_ge(fseq, 4)
                    v.tensor_tensor(parts[:, :, 2], rest[:, 0, :], parts[:, :, 1], ALU.subtract)
                    v.tensor_tensor(parts[:, :, 5], rest[:, 1, :], parts[:, :, 4], ALU.subtract).then_inc(pieces, 1)
                    scale_group(1)
                    v.tensor_scalar(fsc[:], big[:, 2:3], th[:, 1:2], 1.0 / G_SCALE, ALU.mult, ALU.mult)
                    group(0, first=True)
                    with dve.Fori(1, NG - 2) as g:
                        group(g)
                    group(NG - 2, norm_ahead=False)
                    group(NG - 1, final=True, norm_ahead=False)


def kernel(**inputs):
    import numpy as np
    import concourse.bacc as bacc
    from concourse.bass_utils import run_bass_kernel_spmd

    def a(name):
        return np.asarray(inputs[name])

    def turned(name):
        return np.ascontiguousarray(a(name).T)

    fc = turned("L0_ffn_W_fc").reshape(DB, P, 2, CW).transpose(0, 2, 1, 3).reshape(8, P, CW)
    proj = turned("L0_ffn_W_proj").reshape(8, 2, P, D).transpose(0, 2, 1, 3).reshape(8, P, CW)
    arrays = {
        "x": np.ascontiguousarray(a("x")),
        "ctx_t": np.ascontiguousarray(a("ctx_1024").reshape(B * S, D).T),
        "wq_t": turned("L0_xattn_w_q"), "wk_t": turned("L0_xattn_w_k"),
        "wv_t": turned("L0_xattn_w_v"), "wo_t": turned("L0_xattn_w_o"),
        "w_ffn": np.ascontiguousarray(np.concatenate([fc, proj])),
        "lnw": np.ascontiguousarray(a("L0_ffn_ln_w").reshape(HB, P).T),
        "lnb": np.ascontiguousarray(a("L0_ffn_ln_b").reshape(HB, P).T),
        "gates": np.ascontiguousarray(np.broadcast_to(np.stack([a("g_xattn")[0], a("g_ffn")[0]]), (P, 2))),
    }
    nc = bacc.Bacc("TRN2", target_bir_lowering=False, num_devices=1)
    args = [nc.dram_tensor(n, v.shape, mybir.dt.from_np(v.dtype), kind="ExternalInput").ap() for n, v in arrays.items()]
    out = nc.dram_tensor("out", (B, T, D), mybir.dt.float32, kind="ExternalOutput").ap()
    build(nc, *args, out)
    r = run_bass_kernel_spmd(nc, [arrays], core_ids=[0])
    return r.results[0]["out"]
```

```python
import concourse.bass as bass
from concourse import mybir
from contextlib import ExitStack

P = 128
B, T, D = 2, 2048, 512
S = 77
NH, HD = 16, 32
HF = 2048
DB = D // P
HB = HF // P
NP = T // P
HS = NH * S
NJ = -(-HS // P)
HPB = P // HD
VW = HD + 1
NCHUNK = 16
CW = 2 * HF * D // P // NCHUNK
GT = 4
NG = 2 * NP // GT
LN_EPS = 1e-5
GAMMA_EPS = 1e-6

X_SCALE = 2.0 ** 11
W_SCALE = 2.0 ** 15
Q_SHIFT = 2.0 ** -20
P_SCALE = 2.0 ** 12
G_SCALE = 2.0 ** 6

QKV_ORDER = ((0, 0), (0, 1), (1, 0))


def heads_of(j):
    return P * j // S, min((P * j + P - 1) // S, NH - 1)


def build(nc, x, ctx_t, wq_t, wk_t, wv_t, wo_t, w_ffn, lnw, lnb, gates, out):
    f32, f16, bf16 = mybir.dt.float32, mybir.dt.float16, mybir.dt.bfloat16
    ALU = mybir.AluOpType
    ACT = mybir.ActivationFunctionType
    AX = mybir.AxisListType
    ds = bass.ds

    x_v = x.rearrange("b (i p) d -> p i b d", p=P)
    out_v = out.rearrange("b (i p) d -> p i b d", p=P)
    blocks = "(k p) n -> p k n"

    keep = ExitStack()
    with keep:
        def sb(stack, name, shape, dt=f32):
            return stack.enter_context(nc.sbuf_tensor(name, shape, dt))

        def bank(stack, name, n=1):
            return stack.enter_context(nc.psum_tensor(name, [P, n * 512], f32))

        def sem(name):
            return keep.enter_context(nc.semaphore(name))

        xs = sb(keep, "xs", [P, NP, 2, D])
        wt = sb(keep, "wt", [P, NCHUNK, CW], f16)
        wfc = wt[:, 0:8, :].rearrange("p (k a) n -> p k (a n)", k=DB)
        wpr = wt[:, 8:16, :].rearrange("p k (a n) -> p (k a) n", a=2)
        ident = sb(keep, "ident", [P, P])
        ones = sb(keep, "ones", [P, P])
        thr = sb(keep, "thr", [P, 2, 2])
        thr_c = sb(keep, "thr_c", [P, NCHUNK, 2])
        th = sb(keep, "th", [P, 2])
        lnw_s = sb(keep, "lnw_s", [P, HB])
        lnb_s = sb(keep, "lnb_s", [P, HB])
        big = sb(keep, "big", [P, 8])
        inv = sb(keep, "inv", [P, 8])
        pad = sb(keep, "pad", [P, 1])
        pool_pad = sb(keep, "pool_pad", [P, 1])
        xn = sb(keep, "xn", [P, 2, D])
        st = sb(keep, "st", [P, 2, 6])
        mv = sb(keep, "mv", [P, 2, 2])
        ve = sb(keep, "ve", [P, 2])
        rs = sb(keep, "rs", [P, 2])
        NT = 2 * NP
        xs_tiles = xs[:].rearrange("p i s d -> p (i s) d")
        g_xn = sb(keep, "g_xn", [P, GT, D])
        g_st = sb(keep, "g_st", [P, GT, 6])
        g_mv = sb(keep, "g_mv", [P, GT, 2])
        g_ve = sb(keep, "g_ve", [P, GT])
        g_xt = sb(keep, "g_xt", [P, 2, DB, GT * P], f16)
        g_rs = sb(keep, "g_rs", [P, GT])
        aseq, ve_ready, rs_ready, xn_ready = (sem("a_" + n) for n in ("ln_seq", "ve_ready", "rs_ready", "xn_ready"))
        s_x1 = sem("x1_loaded")
        pieces, fseq = sem("f_pieces_made"), sem("f_dve_seq")
        gseq, g_ve_ready, g_rs_ready, g_xn_ready, g_xt_prod, g_xt_hi, g_xt_ready = (sem("f_" + n) for n in (
            "ln_seq", "ve_ready", "rs_ready", "xn_ready", "xt_product", "xt_hi", "xt_ready"))

        def norm_x(i):
            for s in range(2):
                last = nc.vector.bn_stats(st[:, s, :], xs[:, ds(i, 1), s, :].rearrange("p a n -> p (a n)"))
            last.then_inc(aseq, 1)
            nc.vector.wait_ge(aseq, 2 * i + 1)
            nc.vector.memset(pad[:], 0.0)
            for s in range(2):
                last = nc.vector.bn_aggr(mv[:, s, :], st[:, s, :])
            last.then_inc(aseq, 1)
            nc.vector.wait_ge(aseq, 2 * i + 2)
            nc.vector.tensor_scalar(ve[:], mv[:, :, 1], LN_EPS, X_SCALE ** -2, ALU.add, ALU.mult).then_inc(ve_ready, 1)

        def scale_x(i):
            nc.vector.wait_ge(rs_ready, i + 1)
            for s in range(2):
                nc.vector.tensor_scalar(xn[:, s, :], xs[:, ds(i, 1), s, :].rearrange("p a n -> p (a n)"),
                                        mv[:, s, 0:1], rs[:, s:s + 1], ALU.subtract, ALU.mult).then_inc(xn_ready, 1)

        def norm_group(g, tiles=range(GT), rest=True):
            for tt in tiles:
                last = nc.vector.bn_stats(g_st[:, tt, :], xs_tiles[:, ds(GT * g + tt, 1), :].rearrange("p a n -> p (a n)"))
            if not rest:
                return
            last.then_inc(gseq, 1)
            nc.vector.wait_ge(gseq, 2 * g + 1)
            nc.vector.memset(pad[:], 0.0)
            for tt in range(GT):
                last = nc.vector.bn_aggr(g_mv[:, tt, :], g_st[:, tt, :])
            last.then_inc(gseq, 1)
            nc.vector.wait_ge(gseq, 2 * g + 2)
            nc.vector.tensor_scalar(g_ve[:], g_mv[:, :, 1], LN_EPS, X_SCALE ** -2, ALU.add, ALU.mult).then_inc(g_ve_ready, 1)

        def scale_group(g, tiles=range(GT)):
            nc.vector.wait_ge(g_rs_ready, g + 1)
            for tt in tiles:
                nc.vector.tensor_scalar(g_xn[:, tt, :], xs_tiles[:, ds(GT * g + tt, 1), :].rearrange("p a n -> p (a n)"),
                                        g_mv[:, tt, 0:1], g_rs[:, tt:tt + 1], ALU.subtract, ALU.mult).then_inc(g_xn_ready, 1)
        wsc = sb(keep, "wsc", [P, HB])
        parts = sb(keep, "parts", [P, HB, 6], bf16)
        rest = sb(keep, "rest", [P, 2, HB])
        neg_half = sb(keep, "neg_half", [P, 8])

        att = ExitStack()
        with att:
            wq = sb(att, "wq", [P, 2, DB, D], f16)
            wo = sb(att, "wo", [P, 2, DB, D], f16)
            kd = sb(att, "kd", [P, 2, 2, HS], f16)
            vd = sb(att, "vd", [P, 2, 2, NJ, 3 * VW], f16)
            xt = sb(att, "xt", [P, 2, DB, 2 * P], f16)
            q = sb(att, "q", [P, 2, DB, 2 * P], f16)
            esc = sb(att, "esc", [P, 1])
            sc = sb(att, "sc", [P, 8])
            osc = sb(att, "osc", [P, 1])

            psum = att.enter_context(nc.psum_tensor("psum", [P, 8 * 512], f32))
            sc_ps = psum[:, 0:3 * 512]
            V1, T0, T1, X0, V0 = (psum[:, 512 * n:512 * (n + 1)] for n in range(3, 8))

            x_in, xt_prod, xt_hi, xt_ready, q_prod, q_hi, q_ready, sc_prod = (sem("a_" + n) for n in (
                "x_in", "xt_product", "xt_hi", "xt_ready", "q_product", "q_hi", "q_ready", "scores_product"))

            wraw = wt[:].rearrange("p k n -> p (k n)").bitcast(f32).rearrange("p (w k n) -> p w k n", w=4, k=DB)
            wq_r, wk_r, wv_r, wo_r = (wraw[:, n] for n in range(4))


            def transpose_x(i, s, to):
                nc.tensor.wait_ge(xn_ready, 2 * i + s + 1)
                for k in range(DB):
                    last = nc.tensor.transpose(to[:, k * P:(k + 1) * P], xn[:, s, k * P:(k + 1) * P], ident[:])
                last.then_inc(xt_prod, 1)

            def project_q(i, half, to, blocks=(0, 1)):
                nc.tensor.wait_ge(xt_ready, 2 * i + 2)
                for t in (2 * half + k for k in blocks):
                    for n, (a, b) in enumerate(QKV_ORDER):
                        for k in range(DB):
                            last = nc.tensor.matmul(to[:, (t % 2) * 2 * P:(t % 2 + 1) * 2 * P],
                                                    wq[:, a, k, t * P:(t + 1) * P], xt[:, b, k, :],
                                                    start=(n == 0 and k == 0), stop=(n == 2 and k == DB - 1))
                if 1 in blocks:
                    last.then_inc(q_prod, 1)

            def scores(i, s, to):
                nc.tensor.wait_ge(q_ready, 2 * i + 2)
                for t in range(DB):
                    c0, c1 = t * HPB * S, (t + 1) * HPB * S
                    cut = [c0] + [c for c in (512, 1024) if c0 < c < c1] + [c1]
                    for lo, hi in zip(cut, cut[1:]):
                        for n, (a, b) in enumerate(QKV_ORDER):
                            last = nc.tensor.matmul(to[:, lo:hi], q[:, a, t, s * P:(s + 1) * P], kd[:, b, s, lo:hi],
                                                    start=(n == 0), stop=(n == 2))
                last.then_inc(sc_prod, 1)

            def x_high(i, s, bank_):
                nc.scalar.wait_ge(xt_prod, 2 * i + s + 1)
                nc.scalar.copy(xt[:, 0, :, s * P:(s + 1) * P],
                               bank_[:, :].rearrange("p (k n) -> p k n", k=DB)).then_inc(xt_hi, 1)

            def x_low(i, s, bank_):
                nc.vector.wait_ge(xt_hi, 2 * i + s + 1)
                nc.vector.tensor_tensor(xt[:, 1, :, s * P:(s + 1) * P], bank_[:, :].rearrange("p (k n) -> p k n", k=DB),
                                        xt[:, 0, :, s * P:(s + 1) * P], ALU.subtract).then_inc(xt_ready, 1)

            def q_high(i, half, bank_):
                nc.scalar.wait_ge(q_prod, 2 * i + half + 1)
                nc.scalar.mul(q[:, 0, 2 * half:2 * half + 2, :],
                              bank_[:, :].rearrange("p (t n) -> p t n", t=2), Q_SHIFT).then_inc(q_hi, 1)

            def q_low(i, half, bank_):
                nc.vector.wait_ge(q_hi, 2 * i + half + 1)
                nc.vector.scalar_tensor_tensor(q[:, 1, 2 * half:2 * half + 2, :].rearrange("p t n -> p (t n)"),
                                               bank_[:, :], Q_SHIFT,
                                               q[:, 0, 2 * half:2 * half + 2, :].rearrange("p t n -> p (t n)"),
                                               ALU.mult, ALU.subtract).then_inc(q_ready, 1)

            tmp = ExitStack()
            with tmp:
                cx = sb(tmp, "cx", [P, DB, 2 * S])
                vs = sb(tmp, "vs", [P, 2, 2, NH, VW], f16)
                spread = sb(tmp, "spread", [P, 3, NJ * P], f16)
                ks = sb(tmp, "ks", [P, DB, 2 * S])
                gate = sb(tmp, "gate", [P, 2])
                mx = sb(tmp, "mx", [P, 8])
                guard = sb(tmp, "guard", [P, 8])
                prod = sb(tmp, "prod", [P, 4])
                KS = 256
                k_ps = psum[:, 0:DB * KS].rearrange("p (t n) -> p t n", t=DB)[:, :, 0:2 * S]
                v_ps = psum[0:S, 1024:2048].rearrange("p (b n) -> p b n", b=2)
                ROW_BANKS = (T0, T1, X0, V0)
                X0_BANKS, Q0_BANKS, X1_BANKS = (T0, T1), (X0, V0), (psum[:, 0:512], psum[:, 512:1024])
                NJH = NJ // 2

                s_wq, s_wo, s_wk, s_wv, s_cx, s_small, s_x0 = (sem(n) for n in (
                    "wq_loaded", "wo_loaded", "wk_loaded", "wv_loaded", "ctx_loaded", "small_loaded", "x0_loaded"))
                (ident_made, spread_zero, spread_made, kd_zero, vs_zero, vs_ones, max_q, max_o, max_k, max_v, big_q, big_o, big_k,
                 big_v, k_prod, v_prod, rows_prod, rows_read_a, rows_read_v, qseq, oseq, kseq, vseq, pseq, sc_q, sc_k, sc_v,
                 mx_zero, wq_hi, wq_split, k_scaled, kd_hi, kd_lo, vs_hi, vs_lo, th_done) = (sem("s_" + n) for n in (
                    "ident_made", "spread_zeroed", "spread_made", "kd_zeroed", "vs_zeroed", "vs_ones", "max_wq", "max_wo", "max_k",
                    "max_v", "big_wq", "big_wo", "big_k", "big_v", "k_product", "v_product", "rows_product", "rows_read_act",
                    "rows_read_dve", "wq_seq", "wo_seq", "k_seq", "v_seq", "scales_seq", "wq_scale", "k_scale",
                    "v_scale", "mx_zeroed", "wq_hi", "wq_split", "k_scaled", "kd_hi", "kd_lo", "vs_hi", "vs_lo",
                    "tanh_made"))

                def kd_grid(part, h):
                    return kd[HD * h:HD * (h + 1), part].rearrange("p b (t q s) -> p b t q s", t=DB, q=HPB)[:, :, :, h, :]

                def k_rows(h):
                    return ks[HD * h:HD * (h + 1)].rearrange("p t (b s) -> p b t s", b=2)

                ROWS = [(part, b, half) for part in range(2) for b in range(2) for half in range(2)]

                with nc.Block() as block:
                    @block.sync
                    def _(sp):
                        sp.dma_start(cx[:], ctx_t.rearrange(blocks, p=P)).then_inc(s_cx, 16)
                        sp.dma_start(wk_r, wk_t.rearrange(blocks, p=P)).then_inc(s_wk, 16)
                        sp.dma_start(wq_r, wq_t.rearrange(blocks, p=P)).then_inc(s_wq, 16)
                        sp.dma_start(xs[:, 0], x_v[:, 0]).then_inc(s_x0, 16)
                        sp.dma_start(wv_r, wv_t.rearrange(blocks, p=P)).then_inc(s_wv, 16)
                        sp.dma_start(wo_r, wo_t.rearrange(blocks, p=P)).then_inc(s_wo, 16)
                        sp.dma_start(lnw_s[:], lnw).then_inc(s_small, 16)
                        sp.dma_start(lnb_s[:], lnb).then_inc(s_small, 16)
                        sp.dma_start(gate[:], gates).then_inc(s_small, 16)
                        sp.dma_start(xs[:, 1], x_v[:, 1]).then_inc(s_x1, 16)
                        sp.dma_start(xs[:, 2], x_v[:, 2]).then_inc(x_in, 16)

                    @block.gpsimd
                    def _(pool):
                        g = nc.gpsimd
                        g.memset(ident[:], 0.0)
                        g.memset(ones[:], 1.0)
                        g.memset(neg_half[:], -0.5)
                        g.memset(vs[:], 0.0).then_inc(vs_zero, 1)
                        pool.wait_ge(vs_zero, 1)
                        g.affine_select(out=ident[:], in_=ident[:], compare_op=ALU.not_equal, fill=1.0, base=0,
                                        pattern=[[-1, P]], channel_multiplier=1).then_inc(ident_made, 1)
                        g.memset(vs[:, 0, :, :, HD:VW], W_SCALE).then_inc(vs_ones, 1)
                        for part in range(2):
                            g.memset(kd[:, part].bitcast(f32), 0.0).then_inc(kd_zero, 1)

                        def rstd(i):
                            pool.wait_ge(ve_ready, i + 1)
                            g.tensor_tensor(rs[:], ve[:], neg_half[:, 0:2], ALU.pow).then_inc(rs_ready, 1)

                        def all_max(c0, c1):
                            return g.partition_all_reduce(big[:, c0:c1], mx[:, c0:c1], P, bass.bass_isa.ReduceOp.absmax)

                        pool.wait_ge(max_q, 1)
                        all_max(0, 1).then_inc(big_q, 1)
                        rstd(0)
                        def kd_low(h):
                            pool.wait_ge(kd_hi, h + 1)
                            if h:
                                pool.wait_ge(kd_lo, h)
                            for b in range(2):
                                last = g.tensor_tensor(kd_grid(1, h)[:, b], k_rows(h)[:, b], kd_grid(0, h)[:, b], ALU.subtract)
                            last.then_inc(kd_lo, 1)

                        pool.wait_ge(max_k, 1)
                        all_max(3, 4).then_inc(big_k, 1)
                        pool.wait_ge(big_k, 1)
                        kd_low(0)
                        kd_low(1)
                        pool.wait_ge(kd_lo, 2)
                        pool.wait_ge(max_o, 2)
                        all_max(1, 3).then_inc(big_o, 1)
                        pool.wait_ge(max_v, 1)
                        all_max(4, 5).then_inc(big_v, 1)
                        rstd(1)
                        pool.wait_ge(rs_ready, 2)
                        kd_low(2)
                        kd_low(3)
                        pool.wait_ge(kd_lo, 4)
                        rstd(2)

                    @block.tensor
                    def _(pe):
                        mm = nc.tensor.matmul
                        pe.wait_ge(s_cx, 16)
                        pe.wait_ge(s_wk, 16)
                        for t in range(DB):
                            for k in range(DB):
                                last = mm(k_ps[:, t, :], wk_r[:, k, t * P:(t + 1) * P], cx[:, k, :],
                                          start=(k == 0), stop=(k == DB - 1))
                        last.then_inc(k_prod, 1)
                        pe.wait_ge(ident_made, 1)
                        transpose_x(0, 0, X0_BANKS[0])
                        transpose_x(0, 1, X0_BANKS[1])
                        pe.wait_ge(s_wv, 16)
                        for b in range(2):
                            for k in range(DB):
                                last = mm(v_ps[:, b, :], cx[:, k, b * S:(b + 1) * S], wv_r[:, k, :],
                                          start=(k == 0), stop=(k == DB - 1))
                        last.then_inc(v_prod, 1)
                        pe.wait_ge(wq_split, 1)
                        project_q(0, 0, Q0_BANKS[0])
                        project_q(0, 1, Q0_BANKS[1])
                        pe.wait_ge(k_scaled, 1)
                        transpose_x(1, 0, X1_BANKS[0])
                        transpose_x(1, 1, X1_BANKS[1])
                        pe.wait_ge(spread_made, 1)
                        pe.wait_ge(q_ready, 2)
                        for n, (part, b, half) in enumerate(ROWS):
                            pe.wait_ge(*((vs_hi, 1) if part == 0 else (vs_lo, 1)))
                            if n >= 4:
                                pe.wait_ge((rows_read_a, rows_read_v)[half], n // 2 - 1)
                            for j in range(NJH * half, NJH * (half + 1)):
                                for slot in range(3):
                                    h = min(heads_of(j)[0] + slot, NH - 1)
                                    last = mm(ROW_BANKS[n % 4][:, (3 * (j - NJH * half) + slot) * VW:][:, 0:VW],
                                              spread[0:S, slot, P * j:P * (j + 1)], vs[0:S, part, b, h, :], start=True, stop=True)
                            last.then_inc(rows_prod, 1)
                        pe.wait_ge(kd_lo, HPB)
                        pe.wait_ge(xt_ready, 4)
                        scores(0, 0, sc_ps)

                    @block.scalar
                    def _(act):
                        a = nc.scalar
                        act.wait_ge(sc_q, 1)
                        a.activation(wq[:, 0], wq_r, ACT.Copy, scale=sc[:, 0:1]).then_inc(wq_hi, 1)
                        x_high(0, 0, X0_BANKS[0])
                        x_high(0, 1, X0_BANKS[1])
                        act.wait_ge(sc_k, 1)
                        a.activation(ks[:], k_ps, ACT.Copy, scale=sc[:, 3:4]).then_inc(k_scaled, 1)
                        act.wait_ge(k_scaled, 1)
                        act.wait_ge(kd_zero, 2)
                        for h in range(HPB):
                            a.copy(kd_grid(0, h), k_rows(h)).then_inc(kd_hi, 1)
                        act.wait_ge(s_small, 48)
                        a.activation(th[:], gate[:], ACT.Tanh).then_inc(th_done, 1)
                        act.wait_ge(sc_v, 1)
                        act.wait_ge(vs_ones, 1)
                        a.activation(vs[0:S, 0, :, :, 0:HD], v_ps.rearrange("p b (h c) -> p b h c", c=HD), ACT.Copy,
                                     scale=sc[0:S, 4:5]).then_inc(vs_hi, 1)
                        q_high(0, 0, Q0_BANKS[0])
                        q_high(0, 1, Q0_BANKS[1])
                        x_high(1, 0, X1_BANKS[0])
                        x_high(1, 1, X1_BANKS[1])
                        for n, (part, b, half) in enumerate(ROWS):
                            if half == 0:
                                act.wait_ge(rows_prod, n + 1)
                                a.copy(vd[:, part, b, 0:NJH].rearrange("p j c -> p (j c)"),
                                       ROW_BANKS[n % 4][:, 0:NJH * 3 * VW]).then_inc(rows_read_a, 1)
                        a.activation(wo_r, wo_r, ACT.Copy, scale=sc[:, 1:2])

                    @block.vector
                    def _(dve):
                        v = nc.vector

                        def scale_of(c0, c1, seq):
                            v.tensor_scalar(guard[:, c0:c1], big[:, c0:c1], 1e-30, None, ALU.max).then_inc(seq, 1)
                            dve.wait_ge(seq, 1)
                            v.reciprocal(inv[:, c0:c1], guard[:, c0:c1]).then_inc(seq, 1)
                            dve.wait_ge(seq, 2)
                            return v.tensor_scalar(sc[:, c0:c1], inv[:, c0:c1], W_SCALE, None, ALU.mult)

                        def w_low(w, raw, scale):
                            return v.scalar_tensor_tensor(w[:, 1].rearrange("p k n -> p (k n)"), raw.rearrange("p k n -> p (k n)"),
                                                          scale, w[:, 0].rearrange("p k n -> p (k n)"), ALU.mult, ALU.subtract)

                        def max_of(c, values):
                            return v.tensor_reduce(mx[0:values.shape[0], c:c + 1], values, AX.XY, ALU.max, apply_absolute_value=True)

                        v.memset(mx[:], 0.0).then_inc(mx_zero, 1)
                        v.memset(spread[:].bitcast(f32), 0.0).then_inc(spread_zero, 1)
                        dve.wait_ge(ident_made, 1)
                        dve.wait_ge(spread_zero, 1)
                        for j in range(NJ):
                            for slot in range(3):
                                r = S * (heads_of(j)[0] + slot) - P * j
                                r0, r1 = max(r, 0), min(r + S, P, HS - P * j)
                                if r1 > r0:
                                    last = v.tensor_copy(spread[:, slot, P * j + r0:P * j + r1], ident[:, r0 - r:r1 - r])
                        last.then_inc(spread_made, 1)
                        dve.wait_ge(mx_zero, 1)
                        dve.wait_ge(s_wq, 16)
                        max_of(0, wq_r).then_inc(max_q, 1)
                        dve.wait_ge(s_x0, 16)
                        norm_x(0)
                        dve.wait_ge(big_q, 1)
                        scale_of(0, 1, qseq).then_inc(sc_q, 1)
                        scale_x(0)
                        dve.wait_ge(k_prod, 1)
                        max_of(3, k_ps).then_inc(max_k, 1)
                        dve.wait_ge(big_k, 1)
                        scale_of(3, 4, kseq).then_inc(sc_k, 1)
                        dve.wait_ge(wq_hi, 1)
                        w_low(wq, wq_r, sc[:, 0:1]).then_inc(wq_split, 1)
                        x_low(0, 0, X0_BANKS[0])
                        x_low(0, 1, X0_BANKS[1])
                        dve.wait_ge(s_wo, 16)
                        max_of(1, wo_r).then_inc(max_o, 1)
                        dve.wait_ge(s_small, 48)
                        v.tensor_reduce(mx[:, 2:3], lnw_s[:], AX.X, ALU.max, apply_absolute_value=True).then_inc(max_o, 1)
                        dve.wait_ge(v_prod, 1)
                        max_of(4, v_ps).then_inc(max_v, 1)
                        dve.wait_ge(big_o, 1)
                        scale_of(1, 3, oseq)
                        dve.wait_ge(s_x1, 16)
                        norm_x(1)
                        dve.wait_ge(big_v, 1)
                        scale_of(4, 5, vseq).then_inc(sc_v, 1)
                        scale_x(1)
                        dve.wait_ge(vs_hi, 1)
                        for b in range(2):
                            last = v.scalar_tensor_tensor(vs[0:S, 1, b, :, 0:HD], v_ps[:, b, :].rearrange("p (h c) -> p h c", c=HD),
                                                          sc[0:S, 4:5], vs[0:S, 0, b, :, 0:HD], ALU.mult, ALU.subtract)
                        last.then_inc(vs_lo, 1)
                        q_low(0, 0, Q0_BANKS[0])
                        q_low(0, 1, Q0_BANKS[1])
                        x_low(1, 0, X1_BANKS[0])
                        x_low(1, 1, X1_BANKS[1])
                        for n, (part, b, half) in enumerate(ROWS):
                            if n == 5:
                                dve.wait_ge(x_in, 16)
                                norm_x(2)
                            if half == 1:
                                dve.wait_ge(rows_prod, n + 1)
                                v.tensor_copy(vd[:, part, b, NJH:NJ].rearrange("p j c -> p (j c)"),
                                              ROW_BANKS[n % 4][:, 0:NJH * 3 * VW]).then_inc(rows_read_v, 1)
                        scale_x(2)
                        dve.wait_ge(th_done, 1)
                        v.tensor_tensor(prod[:, 0:1], big[:, 0:1], big[:, 3:4], ALU.mult)
                        v.tensor_tensor(prod[:, 1:2], big[:, 1:2], big[:, 4:5], ALU.mult).then_inc(pseq, 1)
                        dve.wait_ge(pseq, 1)
                        v.tensor_scalar(esc[:], prod[:, 0:1], HD ** -0.5 / (X_SCALE * W_SCALE * Q_SHIFT * W_SCALE), None, ALU.mult)
                        v.tensor_scalar(osc[:], prod[:, 1:2], th[:, 0:1], 1.0 / (W_SCALE * W_SCALE), ALU.mult, ALU.mult)

            run = ExitStack()
            with run:
                pr = sb(run, "pr", [P, 2, NJ * P])
                mxs = sb(run, "mxs", [P, 2, NH])
                pt = sb(run, "pt", [P, 2, 2, NJ * P], f16)
                rc = sb(run, "rc", [P, 2, NH])
                o = sb(run, "o", [P, 2, D])
                ot = sb(run, "ot", [P, 2, 2, DB, P], f16)
                wc = [sb(run, f"wc{k}", [P, CW]) for k in range(2)]
                wf = wt[:].rearrange("p k n -> p (k n)").bitcast(f32).rearrange("p (k a n) -> p k a n", k=4, a=2)
                asum = sb(run, "asum", [P, 8])
                asum2 = sb(run, "asum2", [P, 2])
                PW = 4
                wa = sb(run, "wa", [P, CW])
                wb = sb(run, "wb", [P, CW])
                tc = sb(run, "tc", [P, 2])
                PT_BANKS = ((T0, T1, X0), (T1, X0, V0))
                SC_LAST = psum[:, 3 * 512:6 * 512]
                PT_LAST = tuple(sc_ps[:, 512 * n:512 * (n + 1)] for n in range(3))
                PT_BLOCKS = ((0, 4), (4, 8), (8, NJ))
                PV_BANKS = ((V1, T0), (X0, V0))
                PV_BOTH = [psum[:, 512 * n:512 * (n + 2)].rearrange("p (a c) -> p a c", a=2)[:, :, 0:8 * VW].rearrange(
                    "p a (h c) -> p a h c", h=8) for n in (3, 6)]
                OT_BANKS = (T0, X0)
                O_BANKS = (T0, V0)

                (maxd, shifted,
                 expd, pt_prod, pt_hi, pt_ready, pv_prod, rcp, normed, ot_prod, ot_hi, ot_ready, o_prod, x_done,
                 wo_hi, wo_lo, abs_done, asum_done, g_prod, tseq, thr_made, w_cmp, w_done, t_cur, pr_zero) = (sem("a_" + n) for n in (
                    "maxima", "scores_shifted", "exp_done", "pt_product", "pt_hi", "pt_ready",
                    "pv_product", "rcp_done", "o_normed", "ot_product", "ot_hi", "ot_ready", "o_product", "x_done",
                    "wo_hi", "wo_lo", "abs_done", "abs_sums_added", "gamma_product", "threshold_seq", "thresholds_made", "w_compared", "w_done", "threshold_set", "pr_zeroed"))
                w_in, wf_in = ([sem(f"a_{n}{k}") for k in range(2)] for n in ("w_in", "wf_in"))


                with nc.Block() as block:
                    @block.sync
                    def _(sp):
                        def load_x(i):
                            sp.dma_start(xs[:, ds(i, 1)], x_v[:, ds(i, 1)]).then_inc(x_in, 16)

                        def load_sum(c):
                            if c >= 2:
                                sp.wait_ge(abs_done, c - 1)
                            sp.dma_start(wf[:, c % 2], w_ffn[2 * c:2 * c + 2].rearrange("c p n -> p c n")).then_inc(wf_in[c % 2], 16)

                        def load_chunk(c, k):
                            sp.dma_start(wc[k][:], w_ffn[ds(c, 1)].rearrange("c p n -> p (c n)")).then_inc(w_in[k], 16)

                        load_x(3)
                        load_sum(0)
                        load_sum(1)
                        load_chunk(0, 0)
                        load_chunk(1, 1)
                        for c in range(2, 2 * PW):
                            sp.wait_ge(x_in, 16 * c)
                            load_x(c + 2)
                            load_sum(c)
                        with sp.Fori(2 * PW + 2, NP) as i:
                            sp.wait_ge(x_in, 16 * i - 32)
                            load_x(i)
                        with sp.Fori(0, NCHUNK // 2 - 1) as m:
                            for k in range(2):
                                sp.wait_ge(w_done, 2 * m + k + 1)
                                load_chunk(2 * m + k + 2, k)

                    @block.gpsimd
                    def _(pool):
                        g = nc.gpsimd

                        def carry_wait():
                            g.tensor_tensor(pool_pad[:], neg_half[:, 0:1], neg_half[:, 1:2], ALU.mult)

                        def rstd(i):
                            pool.wait_ge(ve_ready, i + 1)
                            g.tensor_tensor(rs[:], ve[:], neg_half[:, 0:2], ALU.pow).then_inc(rs_ready, 1)

                        def ternarize(m, k):
                            i = 2 * m + k
                            pool.wait_ge(w_in[k], 16 * m + 16)
                            carry_wait()
                            g.tensor_copy(tc[:], thr_c[:, ds(i, 1), :].rearrange("p a b -> p (a b)")).then_inc(t_cur, 1)
                            pool.wait_ge(t_cur, i + 1)
                            carry_wait()
                            g.tensor_scalar(wa[:], wc[k][:], tc[:, 0:1], None, ALU.is_gt)
                            g.tensor_scalar(wb[:], wc[k][:], tc[:, 1:2], None, ALU.is_lt).then_inc(w_cmp, 1)
                            pool.wait_ge(w_cmp, i + 1)
                            g.tensor_tensor(wt[:, ds(i, 1), :].rearrange("p a n -> p (a n)"), wa[:], wb[:],
                                            ALU.subtract).then_inc(w_done, 1)

                        pool.wait_ge(wo_hi, 1)
                        g.tensor_tensor(wo[:, 1].rearrange("p k n -> p (k n)"), wo_r.rearrange("p k n -> p (k n)"),
                                        wo[:, 0].rearrange("p k n -> p (k n)"), ALU.subtract).then_inc(wo_lo, 1)
                        for i in range(PW):
                            rstd(i + 3)
                        pool.wait_ge(thr_made, 1)
                        with pool.Fori(0, NCHUNK // 2) as m:
                            rstd(m + PW + 3)
                            ternarize(m, 0)
                            ternarize(m, 1)
                        for i in range(NCHUNK // 2 + PW + 3, NP):
                            rstd(i)
                        for k in range(2):
                            pool.wait_ge(g_ve_ready, k + 1)
                            g.tensor_tensor(g_rs[:], g_ve[:], neg_half[:, 0:GT], ALU.pow).then_inc(g_rs_ready, 1)

                    @block.tensor
                    def _(pe):
                        mm = nc.tensor.matmul

                        def transpose_p(i, s, banks, final=False):
                            pe.wait_ge(expd, 2 * i + s + 1)
                            for c, (j0, j1) in enumerate(PT_BLOCKS):
                                if s == 1 and c == 2 and not final:
                                    pe.wait_ge(q_ready, 2 * i + 4)
                                if final and c:
                                    pe.wait_ge(g_xt_ready, c)
                                for j in range(j0, j1):
                                    last = nc.tensor.transpose(banks[c][:, (j - j0) * P:(j - j0 + 1) * P],
                                                               pr[:, s, P * j:P * (j + 1)], ident[:])
                                last.then_inc(pt_prod, 1)

                        def weigh_v(i, s):
                            first = [True, True]
                            for j in range(NJ):
                                if j in (0, 4) or j == 8 and s == 0:
                                    pe.wait_ge(pt_ready, 3 * (2 * i + s) + s + j // 4 + 1)
                                h0, h1 = heads_of(j)
                                parts = [(h0, min(h1, 7), 0)] if h0 < 8 else []
                                parts += [(max(h0, 8), h1, 1)] if h1 >= 8 else []
                                for ha, hb, side in parts:
                                    for n, (a, b) in enumerate(QKV_ORDER):
                                        final = n == 2 and (hb == 7 and j == 4 or j == NJ - 1)
                                        last = mm(PV_BANKS[s][side][:, (ha % 8) * VW:(hb % 8 + 1) * VW],
                                                  pt[:, s, a, P * j:P * (j + 1)],
                                                  vd[:, b, s, j, (ha - h0) * VW:(hb - h0 + 1) * VW],
                                                  start=first[side], stop=final, skip_group_check=True)
                                        first[side] = False
                            last.then_inc(pv_prod, 1)

                        def transpose_o(i, s):
                            pe.wait_ge(normed, 2 * i + s + 1)
                            for k in range(DB):
                                last = nc.tensor.transpose(OT_BANKS[s][:, k * P:(k + 1) * P], o[:, s, k * P:(k + 1) * P], ident[:])
                            last.then_inc(ot_prod, 1)

                        def project_o(i, s):
                            pe.wait_ge(ot_ready, 2 * i + s + 1)
                            for n, (a, b) in enumerate(QKV_ORDER):
                                for k in range(DB):
                                    last = mm(O_BANKS[s][:, :], ot[:, s, a, k, :], wo[:, b, k, :],
                                              start=(n == 0 and k == 0), stop=(n == 2 and k == DB - 1))
                            last.then_inc(o_prod, 1)

                        def transpose_group(tt, to):
                            pe.wait_ge(g_xn_ready, tt + 1)
                            for k in range(DB):
                                last = nc.tensor.transpose(to[:, k * P:(k + 1) * P], g_xn[:, tt, k * P:(k + 1) * P], ident[:])
                            last.then_inc(g_xt_prod, 1)

                        def one_pair(i, first=False, q_ahead=True, x_ahead=True, gammas=False):
                            if not first:
                                pe.wait_ge(shifted, 2 * i)
                                scores(i, 0, sc_ps)
                            if not q_ahead:
                                pe.wait_ge(x_done, 2 * i - 1)
                                scores(i, 1, SC_LAST)
                            if not first:
                                project_o(i - 1, 1)
                            if gammas:
                                pe.wait_ge(asum_done, 1)
                                pe.wait_ge(xt_ready, 2 * i + 4)
                                mm(T1[:, 0:2], ones[:], asum2[:], start=True, stop=True).then_inc(g_prod, 1)
                            if q_ahead:
                                project_q(i + 1, 0, V1, (0,))
                                pe.wait_ge(shifted, 2 * i + 1)
                                scores(i, 1, sc_ps)
                                project_q(i + 1, 0, V1, (1,))
                                if not first:
                                    pe.wait_ge(x_done, 2 * i - 1)
                                if gammas:
                                    pe.wait_ge(thr_made, 1)
                                transpose_p(i, 0, PT_BANKS[0])
                                if not first:
                                    pe.wait_ge(x_done, 2 * i)
                                project_q(i + 1, 1, V0)
                                pe.wait_ge(q_ready, 2 * i + 3)
                                weigh_v(i, 0)
                                transpose_p(i, 1, PT_BANKS[1])
                            else:
                                transpose_p(i, 0, PT_LAST)
                                transpose_group(0, X0)
                                pe.wait_ge(shifted, 2 * i + 2)
                                weigh_v(i, 0)
                                pe.wait_ge(x_done, 2 * i)
                                transpose_group(1, V0)
                                transpose_p(i, 1, PT_BANKS[1], final=True)
                            transpose_o(i, 0)
                            if x_ahead or not q_ahead:
                                if x_ahead:
                                    transpose_x(i + 2, 0, V1)
                                else:
                                    transpose_group(2, V1)
                                pe.wait_ge(pt_ready, 3 * (2 * i + 1) + 1)
                                if x_ahead:
                                    transpose_x(i + 2, 1, T1)
                                else:
                                    transpose_group(3, T1)
                            weigh_v(i, 1)
                            if first:
                                pe.wait_ge(wo_lo, 1)
                            project_o(i, 0)
                            transpose_o(i, 1)

                        pe.wait_ge(pr_zero, 1)
                        one_pair(0, first=True)
                        with pe.Fori(1, PW) as i:
                            one_pair(i)
                        one_pair(PW, gammas=True)
                        with pe.Fori(PW + 1, NP - 2) as i:
                            one_pair(i)
                        one_pair(NP - 2, x_ahead=False)
                        one_pair(NP - 1, q_ahead=False, x_ahead=False)
                        project_o(NP - 1, 1)

                    @block.scalar
                    def _(act):
                        a = nc.scalar

                        def exp(i, s):
                            act.wait_ge(shifted, 2 * i + s + 1)
                            a.activation(pr[:, s, 0:HS], pr[:, s, 0:HS], ACT.Exp, scale=esc[:]).then_inc(expd, 1)

                        def p_high(i, s, banks):
                            for c, (j0, j1) in enumerate(PT_BLOCKS):
                                act.wait_ge(pt_prod, 3 * (2 * i + s) + c + 1)
                                a.mul(pt[:, s, 0, P * j0:P * j1], banks[c][:, 0:P * (j1 - j0)], P_SCALE).then_inc(pt_hi, 1)

                        def o_high(i, s):
                            act.wait_ge(ot_prod, 2 * i + s + 1)
                            a.mul(ot[:, s, 0].rearrange("p k n -> p (k n)"), OT_BANKS[s][:, :], W_SCALE).then_inc(ot_hi, 1)

                        def group_high(tt, bank_):
                            act.wait_ge(g_xt_prod, tt + 1)
                            a.copy(g_xt[:, 0, :, tt * P:(tt + 1) * P], bank_.rearrange("p (k n) -> p k n", k=DB)).then_inc(g_xt_hi, 1)

                        def abs_sum(i, k):
                            act.wait_ge(wf_in[k], 16 * i + 16)
                            a.activation(wf[:, k], wf[:, k], ACT.Abs,
                                         accum_out=asum[:, 2 * i + k:2 * i + k + 1]).then_inc(abs_done, 1)

                        def one_pair(i, q_ahead=True, x_ahead=True, sums=False):
                            exp(i, 0)
                            if sums and i:
                                abs_sum(i, 0)
                            if q_ahead:
                                q_high(i + 1, 0, V1)
                            p_high(i, 0, PT_BANKS[0] if q_ahead else PT_LAST)
                            exp(i, 1)
                            if not q_ahead:
                                group_high(0, X0)
                                group_high(1, V0)
                            if q_ahead:
                                q_high(i + 1, 1, V0)
                            p_high(i, 1, PT_BANKS[1])
                            o_high(i, 0)
                            if x_ahead:
                                x_high(i + 2, 0, V1)
                                x_high(i + 2, 1, T1)
                            if not q_ahead:
                                group_high(2, V1)
                                group_high(3, T1)
                            if sums:
                                abs_sum(i, 1 if i else 0)
                            o_high(i, 1)
                            if sums and not i:
                                abs_sum(i, 1)

                        a.copy(wo[:, 0], wo_r).then_inc(wo_hi, 1)
                        for i in range(PW):
                            one_pair(i, sums=True)
                        with act.Fori(PW, NP - 2) as i:
                            one_pair(i)
                        one_pair(NP - 2, x_ahead=False)
                        one_pair(NP - 1, q_ahead=False, x_ahead=False)

                    @block.vector
                    def _(dve):
                        v = nc.vector

                        def shift_scores(i, s, banks=sc_ps):
                            dve.wait_ge(sc_prod, 2 * i + s + 1)
                            grid = banks[:, 0:HS].rearrange("p (h k) -> p h k", h=NH)
                            v.tensor_reduce(mxs[:, s, :], grid, AX.X, ALU.max).then_inc(maxd, 1)
                            dve.wait_ge(maxd, 2 * i + s + 1)
                            v.tensor_tensor(pr[:, s, 0:HS].rearrange("p (h k) -> p h k", h=NH), grid,
                                            mxs[:, s, :].unsqueeze(2).broadcast_to([P, NH, S]), ALU.subtract).then_inc(shifted, 1)

                        def p_low(i, s, banks):
                            for c, (j0, j1) in enumerate(PT_BLOCKS):
                                dve.wait_ge(pt_hi, 3 * (2 * i + s) + c + 1)
                                v.scalar_tensor_tensor(pt[:, s, 1, P * j0:P * j1], banks[c][:, 0:P * (j1 - j0)], P_SCALE,
                                                       pt[:, s, 0, P * j0:P * j1], ALU.mult, ALU.subtract).then_inc(pt_ready, 1)

                        def norm_o(i, s):
                            dve.wait_ge(pv_prod, 2 * i + s + 1)
                            sums, values = PV_BOTH[s][:, :, :, HD], PV_BOTH[s][:, :, :, 0:HD]
                            v.reciprocal(rc[:, s, :].rearrange("p (a h) -> p a h", a=2), sums).then_inc(rcp, 1)
                            dve.wait_ge(rcp, 2 * i + s + 1)
                            v.tensor_tensor(o[:, s, :].rearrange("p (a h c) -> p a h c", a=2, h=8), values,
                                            rc[:, s, :].rearrange("p (a h) -> p a h", a=2).unsqueeze(3).broadcast_to([P, 2, 8, HD]),
                                            ALU.mult).then_inc(normed, 1)

                        def o_low(i, s):
                            dve.wait_ge(ot_hi, 2 * i + s + 1)
                            v.scalar_tensor_tensor(ot[:, s, 1].rearrange("p k n -> p (k n)"), OT_BANKS[s][:, :], W_SCALE,
                                                   ot[:, s, 0].rearrange("p k n -> p (k n)"),
                                                   ALU.mult, ALU.subtract).then_inc(ot_ready, 1)

                        def add_branch(i, s):
                            dve.wait_ge(o_prod, 2 * i + s + 1)
                            tile = xs[:, ds(i, 1), s, :].rearrange("p a n -> p (a n)")
                            v.scalar_tensor_tensor(tile, O_BANKS[s][:, :], osc[:], tile, ALU.mult, ALU.add).then_inc(x_done, 1)

                        def group_low(tt, bank_):
                            dve.wait_ge(g_xt_hi, tt + 1)
                            v.tensor_tensor(g_xt[:, 1, :, tt * P:(tt + 1) * P], bank_.rearrange("p (k n) -> p k n", k=DB),
                                            g_xt[:, 0, :, tt * P:(tt + 1) * P], ALU.subtract).then_inc(g_xt_ready, 1)

                        def thresholds():
                            dve.wait_ge(g_prod, 1)
                            v.tensor_scalar(thr[:, 0, :], T1[:, 0:2], 1.0 / (HF * D), GAMMA_EPS, ALU.mult, ALU.add).then_inc(tseq, 1)
                            dve.wait_ge(tseq, 1)
                            v.tensor_scalar(thr[:, 1, :], thr[:, 0, :], -0.5, None, ALU.mult).then_inc(tseq, 1)
                            dve.wait_ge(tseq, 2)
                            v.tensor_scalar(thr[:, 0, :], thr[:, 1, :], -1.0, None, ALU.mult).then_inc(tseq, 1)
                            dve.wait_ge(tseq, 3)
                            for w in range(2):
                                last = v.tensor_copy(thr_c[:, 8 * w:8 * w + 8, :],
                                                     thr[:, :, w].unsqueeze(1).broadcast_to([P, 8, 2]))
                            last.then_inc(thr_made, 1)

                        def weight_pieces():
                            v.tensor_scalar(wsc[:], lnw_s[:], inv[:, 2:3], G_SCALE, ALU.mult, ALU.mult).then_inc(fseq, 1)
                            dve.wait_ge(fseq, 1)
                            v.tensor_copy(parts[:, :, 0], wsc[:])
                            v.tensor_copy(parts[:, :, 3], lnb_s[:]).then_inc(fseq, 1)
                            dve.wait_ge(fseq, 2)
                            v.tensor_tensor(rest[:, 0, :], wsc[:], parts[:, :, 0], ALU.subtract)
                            v.tensor_tensor(rest[:, 1, :], lnb_s[:], parts[:, :, 3], ALU.subtract).then_inc(fseq, 1)
                            dve.wait_ge(fseq, 3)
                            v.tensor_copy(parts[:, :, 1], rest[:, 0, :])
                            v.tensor_copy(parts[:, :, 4], rest[:, 1, :]).then_inc(fseq, 1)
                            dve.wait_ge(fseq, 4)
                            v.tensor_tensor(parts[:, :, 2], rest[:, 0, :], parts[:, :, 1], ALU.subtract)
                            v.tensor_tensor(parts[:, :, 5], rest[:, 1, :], parts[:, :, 4], ALU.subtract).then_inc(pieces, 1)

                        def one_pair(i, first=False, q_ahead=True, x_ahead=True, norm_ahead=True, gammas=False):
                            if gammas:
                                dve.wait_ge(abs_done, 2 * PW)
                                v.tensor_reduce(asum2[:], asum[:].rearrange("p (w c) -> p w c", w=2), AX.X, ALU.add).then_inc(asum_done, 1)
                            shift_scores(i, 0)
                            if not q_ahead:
                                shift_scores(i, 1, SC_LAST)
                                p_low(i, 0, PT_LAST)
                            if not first:
                                add_branch(i - 1, 1)
                            if gammas:
                                thresholds()
                            if norm_ahead:
                                dve.wait_ge(x_in, 16 * i + 32)
                                norm_x(i + 3)
                            elif x_ahead:
                                norm_group(0, (0, 1), rest=False)
                            elif q_ahead:
                                norm_group(0, (2, 3))
                            else:
                                scale_group(0, (2, 3))
                                group_low(0, X0)
                            if q_ahead:
                                shift_scores(i, 1)
                                q_low(i + 1, 0, V1)
                                p_low(i, 0, PT_BANKS[0])
                                q_low(i + 1, 1, V0)
                            else:
                                group_low(1, V0)
                            norm_o(i, 0)
                            p_low(i, 1, PT_BANKS[1])
                            o_low(i, 0)
                            if x_ahead:
                                x_low(i + 2, 0, V1)
                                x_low(i + 2, 1, T1)
                            if not q_ahead:
                                group_low(2, V1)
                                group_low(3, T1)
                            norm_o(i, 1)
                            if norm_ahead:
                                scale_x(i + 3)
                            elif x_ahead:
                                weight_pieces()
                            elif q_ahead:
                                scale_group(0, (0, 1))
                            if q_ahead:
                                add_branch(i, 0)
                                o_low(i, 1)
                            else:
                                norm_group(1, (0, 1), rest=False)
                                o_low(i, 1)
                                norm_group(1, (2, 3))
                                add_branch(i, 0)

                        v.memset(pr[:, :, HS:NJ * P], 0.0).then_inc(pr_zero, 1)
                        one_pair(0, first=True)
                        with dve.Fori(1, PW) as i:
                            one_pair(i)
                        one_pair(PW, gammas=True)
                        with dve.Fori(PW + 1, NP - 3) as i:
                            one_pair(i)
                        one_pair(NP - 3, norm_ahead=False)
                        one_pair(NP - 2, x_ahead=False, norm_ahead=False)
                        one_pair(NP - 1, q_ahead=False, x_ahead=False, norm_ahead=False)
                        add_branch(NP - 1, 1)

        ffn = ExitStack()
        with ffn:
            GR = 8
            gf = sb(ffn, "gf", [P, GR, GT * P])
            sq = sb(ffn, "sq", [P, 4, GT * P])
            s12 = sb(ffn, "s12", [P, 2, GT * P])
            gw = sb(ffn, "gw", [P, 2, HB, GT * P], f16)
            zero = sb(ffn, "zero", [P, GT * P])
            colsum = sb(ffn, "colsum", [6, D])
            pick = sb(ffn, "pick", [6, 2, P])
            cw = sb(ffn, "cw", [P, D])
            cb = sb(ffn, "cb", [P, D])
            fsc = sb(ffn, "fsc", [P, 1])
            tot = sb(ffn, "tot", [P, 2, GT])
            negm = sb(ffn, "negm", [P, GT])
            m2 = sb(ffn, "m2", [P, GT])
            ge = sb(ffn, "ge", [P, GT])
            grs = sb(ffn, "grs", [P, GT])
            gr = sb(ffn, "gr", [P, GT])
            t1 = sb(ffn, "t1", [P, 2, D])
            ob = sb(ffn, "ob", [P, 2, D])
            Z = [bank(ffn, f"Z{k}") for k in range(4)]
            R = [bank(ffn, f"R{k}") for k in range(2)]
            XB = bank(ffn, "XB")
            SB = bank(ffn, "SB")
            XT_BANKS = (XB, XB, SB, XB)

            (picked, c6, c6_out, cwb, c_done,
             z_prod, gelu_done, sq_done, s1_done, s2_done, gw_hi_a, gw_hi_v, gw_ready, r_prod, st_prod, sseq, ge_ready, grs_ready,
             r_read, fin, ob_ready, sums_out, x_biased) = (sem("f_" + n) for n in (
                "pick_made", "column_sums", "column_sums_out", "column_sums_bcast", "consts_done",
                "z_product", "gelu_done",
                "sq_done", "s1_done", "s2_done", "gw_hi_act", "gw_hi_dve", "gw_ready", "r_product", "stats_product", "stats_seq", "ge_ready",
                "grs_ready", "r_read", "final_seq", "ob_ready", "sums_out", "x_biased"))
            stored = [sem("f_stored0"), sem("f_stored1")]


            with nc.Block() as block:
                @block.sync
                def _(sp):
                    with sp.Fori(0, NG) as g:
                        for tt in range(GT):
                            sp.wait_ge(ob_ready, GT * g + tt + 1)
                            sp.dma_start(out_v[:, ds(2 * g + tt // 2, 1), tt % 2, :],
                                         ob[:, tt % 2:tt % 2 + 1, :]).then_inc(stored[tt % 2], 16)
                    for k in range(2):
                        sp.wait_ge(stored[k], 16 * NT // 2)

                @block.gpsimd
                def _(pool):
                    g_ = nc.gpsimd
                    g_.memset(zero[:], 0.0)
                    g_.memset(pick[:], 1.0).then_inc(picked, 1)
                    pool.wait_ge(picked, 1)
                    g_.affine_select(out=pick[:, 0, :], in_=pick[:, 0, :], compare_op=ALU.is_ge, fill=0.0, base=2,
                                     pattern=[[0, P]], channel_multiplier=-1)
                    g_.affine_select(out=pick[:, 1, :], in_=pick[:, 1, :], compare_op=ALU.is_ge, fill=0.0, base=-3,
                                     pattern=[[0, P]], channel_multiplier=1).then_inc(picked, 1)

                    def rstd(g):
                        pool.wait_ge(g_ve_ready, g + 1)
                        g_.tensor_tensor(g_rs[:], g_ve[:], neg_half[:, 0:GT], ALU.pow).then_inc(g_rs_ready, 1)

                    def group(g, norm_ahead=True):
                        for h in range(HB):
                            pool.wait_ge(sq_done, HB * g + h + 1)
                            if h == 0:
                                g_.tensor_tensor(s12[:, 1], sq[:, 0], zero[:], ALU.add).then_inc(s2_done, 1)
                            else:
                                pool.wait_ge(s2_done, HB * g + h)
                                g_.tensor_tensor(s12[:, 1], s12[:, 1], sq[:, h % 4], ALU.add).then_inc(s2_done, 1)
                        pool.wait_ge(ge_ready, g + 1)
                        g_.tensor_tensor(grs[:], ge[:], neg_half[:, 0:GT], ALU.pow).then_inc(grs_ready, 1)
                        pool.wait_ge(c_done, 1)
                        pool.wait_ge(g_xn_ready, GT * g + GT)
                        for tt in range(GT):
                            tile = xs_tiles[:, ds(GT * g + tt, 1), :].rearrange("p a n -> p (a n)")
                            g_.tensor_tensor(tile, tile, cb[:], ALU.add).then_inc(x_biased, 1)
                        if norm_ahead:
                            rstd(g + 2)

                    with pool.Fori(0, NG - 2) as g:
                        group(g)
                    group(NG - 2, norm_ahead=False)
                    group(NG - 1, norm_ahead=False)

                @block.tensor
                def _(pe):
                    mm = nc.tensor.matmul

                    def transpose_x(g, tt, to):
                        pe.wait_ge(g_xn_ready, GT * g + tt + 1)
                        for k in range(DB):
                            last = nc.tensor.transpose(to[:, k * P:(k + 1) * P], g_xn[:, tt, k * P:(k + 1) * P], ident[:])
                        last.then_inc(g_xt_prod, 1)

                    def up(g, h, first):
                        if not (first and h < 4):
                            pe.wait_ge(gelu_done, HB * g + h - 3)
                        for k in range(DB):
                            for a in range(2):
                                last = mm(Z[h % 4][:, :], wfc[:, k, h * P:(h + 1) * P], g_xt[:, a, k, :],
                                          start=(k == 0 and a == 0), stop=(k == DB - 1 and a == 1))
                        last.then_inc(z_prod, 1)

                    def down(g, tt, first):
                        if not (first and tt < 2):
                            pe.wait_ge(r_read, GT * g + tt - 1)
                        for h in range(HB):
                            if tt == 0:
                                pe.wait_ge(gw_ready, HB * g + h + 1)
                            for a in range(2):
                                last = mm(R[tt % 2][:, :], gw[:, a, h, tt * P:(tt + 1) * P], wpr[:, h, :],
                                          start=(h == 0 and a == 0), stop=(h == HB - 1 and a == 1))
                        last.then_inc(r_prod, 1)

                    def turn_sums(g, k):
                        for tt in range(GT):
                            last = nc.tensor.transpose((SB, XB)[k][:, tt * P:(tt + 1) * P], s12[:, k, tt * P:(tt + 1) * P], ident[:])
                        last.then_inc(st_prod, 1)

                    def column_sums():
                        pe.wait_ge(pieces, 1)
                        for h in range(HB):
                            last = mm(R[0][0:6, :], parts[:, h, :], wpr[:, h, :], start=(h == 0), stop=(h == HB - 1))
                        last.then_inc(c6, 1)

                    def spread_sums():
                        pe.wait_ge(c6_out, 1)
                        pe.wait_ge(picked, 2)
                        mm(R[1][:, :], pick[:, 0, :], colsum[:], start=True, stop=True)
                        mm(SB[:, :], pick[:, 1, :], colsum[:], start=True, stop=True).then_inc(cwb, 1)

                    def group(g, first=False, final=False):
                        pe.wait_ge(g_xt_ready, GT * g + GT)
                        for h in range(HB):
                            up(g, h, first)
                            if first and h == 8:
                                column_sums()
                            if first and h == 11:
                                spread_sums()
                        if first:
                            pe.wait_ge(c_done, 1)
                        if not final:
                            transpose_x(g + 1, 0, XT_BANKS[0])
                        down(g, 0, first)
                        pe.wait_ge(s1_done, HB * g + HB)
                        turn_sums(g, 0)
                        pe.wait_ge(s2_done, HB * g + HB)
                        if not final:
                            pe.wait_ge(g_xt_ready, GT * g + GT + 1)
                        turn_sums(g, 1)
                        down(g, 1, first)
                        if not final:
                            pe.wait_ge(sums_out, 2 * g + 2)
                            transpose_x(g + 1, 1, XT_BANKS[1])
                            transpose_x(g + 1, 2, XT_BANKS[2])
                        down(g, 2, first)
                        if not final:
                            pe.wait_ge(g_xt_ready, GT * g + GT + 2)
                            transpose_x(g + 1, 3, XT_BANKS[3])
                        down(g, 3, first)

                    group(0, first=True)
                    with pe.Fori(1, NG - 1) as g:
                        group(g)
                    group(NG - 1, final=True)

                @block.scalar
                def _(act):
                    a_ = nc.scalar

                    def x_high(g, tt, bank_):
                        act.wait_ge(g_xt_prod, GT * g + tt + 1)
                        a_.copy(g_xt[:, 0, :, tt * P:(tt + 1) * P], bank_[:, :].rearrange("p (k n) -> p k n", k=DB)).then_inc(g_xt_hi, 1)

                    def square(g, h, first):
                        act.wait_ge(gelu_done, HB * g + h + 1)
                        if not (first and h < 4):
                            act.wait_ge(s2_done, HB * g + h - 3)
                        a_.activation(sq[:, h % 4], gf[:, h % GR], ACT.Square).then_inc(sq_done, 1)

                    def gw_high(g, h, first):
                        if h == 0 and not first:
                            act.wait_ge(r_prod, GT * g)
                        act.wait_ge(gelu_done, HB * g + h + 1)
                        a_.activation(gw[:, 0, h, :], gf[:, h % GR], ACT.Copy, scale=wsc[:, h:h + 1]).then_inc(gw_hi_a, 1)

                    def gelu(g, h, first):
                        act.wait_ge(z_prod, HB * g + h + 1)
                        if not (first and h < GR):
                            act.wait_ge(s1_done, HB * g + h - GR + 1)
                        a_.activation(gf[:, h % GR], Z[h % 4][:, :], ACT.Gelu, scale=1.0 / X_SCALE).then_inc(gelu_done, 1)

                    def group(g, first=False, final=False):
                        for h in range(HB):
                            gelu(g, h, first)
                            if h % 2 == 0:
                                gw_high(g, h, first)
                            if h:
                                square(g, h - 1, first)
                        square(g, HB - 1, first)
                        if not final:
                            for tt in range(GT):
                                x_high(g + 1, tt, XT_BANKS[tt])

                    group(0, first=True)
                    with act.Fori(1, NG - 1) as g:
                        group(g)
                    group(NG - 1, final=True)

                @block.vector
                def _(dve):
                    v = nc.vector

                    def x_low(g, tt, bank_):
                        dve.wait_ge(g_xt_hi, GT * g + tt + 1)
                        v.tensor_tensor(g_xt[:, 1, :, tt * P:(tt + 1) * P], bank_[:, :].rearrange("p (k n) -> p k n", k=DB),
                                        g_xt[:, 0, :, tt * P:(tt + 1) * P], ALU.subtract).then_inc(g_xt_ready, 1)

                    def split_g(g, h, first):
                        dve.wait_ge(gelu_done, HB * g + h + 1)
                        if h % 2:
                            v.tensor_scalar(gw[:, 0, h, :], gf[:, h % GR], wsc[:, h:h + 1], None, ALU.mult).then_inc(gw_hi_v, 1)
                        dve.wait_ge((gw_hi_a, gw_hi_v)[h % 2], HB // 2 * g + h // 2 + 1)
                        v.scalar_tensor_tensor(gw[:, 1, h, :], gf[:, h % GR], wsc[:, h:h + 1], gw[:, 0, h, :],
                                               ALU.mult, ALU.subtract).then_inc(gw_ready, 1)
                        if h == 0:
                            v.tensor_copy(s12[:, 0], gf[:, 0]).then_inc(s1_done, 1)
                        else:
                            dve.wait_ge(s1_done, HB * g + h)
                            v.tensor_tensor(s12[:, 0], s12[:, 0], gf[:, h % GR], ALU.add).then_inc(s1_done, 1)

                    def moments(g):
                        for k in range(2):
                            dve.wait_ge(st_prod, 2 * g + k + 1)
                            v.tensor_reduce(tot[:, k, :], (SB, XB)[k][:, :].rearrange("p (t n) -> p t n", t=GT), AX.X,
                                            ALU.add).then_inc(sums_out, 1)
                        dve.wait_ge(sums_out, 2 * g + 2)
                        v.tensor_scalar(negm[:], tot[:, 0, :], -1.0 / HF, None, ALU.mult).then_inc(sseq, 1)
                        dve.wait_ge(sseq, 3 * g + 1)
                        v.tensor_tensor(m2[:], negm[:], negm[:], ALU.mult).then_inc(sseq, 1)
                        dve.wait_ge(sseq, 3 * g + 2)
                        v.scalar_tensor_tensor(ge[:], tot[:, 1, :], 1.0 / HF, m2[:], ALU.mult, ALU.subtract).then_inc(sseq, 1)
                        dve.wait_ge(sseq, 3 * g + 3)
                        v.tensor_scalar(ge[:], ge[:], 0.0, LN_EPS, ALU.max, ALU.add).then_inc(ge_ready, 1)
                        dve.wait_ge(grs_ready, g + 1)
                        v.tensor_scalar(gr[:], grs[:], fsc[:], None, ALU.mult).then_inc(fin, 1)

                    def finish(g, tt, first):
                        n = GT * g + tt
                        dve.wait_ge(r_prod, n + 1)
                        if tt == 0:
                            dve.wait_ge(fin, g + 1)
                        if not (first and tt < 2):
                            dve.wait_ge(ob_ready, n - 1)
                        v.scalar_tensor_tensor(t1[:, tt % 2, :], cw[:], negm[:, tt:tt + 1], R[tt % 2][:, :], ALU.mult, ALU.add).then_inc(r_read, 1)
                        dve.wait_ge(r_read, n + 1)
                        dve.wait_ge(x_biased, n + 1)
                        if not (first and tt < 2):
                            dve.wait_ge(stored[tt % 2], 16 * (2 * g + tt // 2))
                        v.scalar_tensor_tensor(ob[:, tt % 2, :], t1[:, tt % 2, :], gr[:, tt:tt + 1],
                                               xs_tiles[:, ds(n, 1), :].rearrange("p a n -> p (a n)"), ALU.mult, ALU.add).then_inc(ob_ready, 1)

                    def group(g, first=False, final=False, norm_ahead=True):
                        for h in range(HB):
                            split_g(g, h, first)
                            if first and h == 8:
                                dve.wait_ge(c6, 1)
                                v.tensor_copy(colsum[:], R[0][0:6, :]).then_inc(c6_out, 1)
                            if first and h == 12:
                                dve.wait_ge(cwb, 1)
                                v.tensor_copy(cw[:], R[1][:, :])
                                v.tensor_scalar(cb[:], SB[:, :], th[:, 1:2], None, ALU.mult).then_inc(c_done, 1)
                        if not final:
                            x_low(g + 1, 0, XT_BANKS[0])
                        moments(g)
                        for tt in range(GT):
                            finish(g, tt, first)
                            if not final:
                                for t in {1: (1, 2), 2: (3,)}.get(tt, ()):
                                    x_low(g + 1, t, XT_BANKS[t])
                            if tt == 1 and norm_ahead:
                                norm_group(g + 2)
                        if norm_ahead:
                            scale_group(g + 2)

                    scale_group(1)
                    v.tensor_scalar(fsc[:], big[:, 2:3], th[:, 1:2], 1.0 / G_SCALE, ALU.mult, ALU.mult)
                    group(0, first=True)
                    with dve.Fori(1, NG - 2) as g:
                        group(g)
                    group(NG - 2, norm_ahead=False)
                    group(NG - 1, final=True, norm_ahead=False)


def kernel(**inputs):
    import numpy as np
    import concourse.bacc as bacc
    from concourse.bass_utils import run_bass_kernel_spmd

    def a(name):
        return np.asarray(inputs[name])

    def turned(name):
        return np.ascontiguousarray(a(name).T)

    fc = turned("L0_ffn_W_fc").reshape(DB, P, 2, CW).transpose(0, 2, 1, 3).reshape(8, P, CW)
    proj = turned("L0_ffn_W_proj").reshape(8, 2, P, D).transpose(0, 2, 1, 3).reshape(8, P, CW)
    arrays = {
        "x": np.ascontiguousarray(a("x")),
        "ctx_t": np.ascontiguousarray(a("ctx_1024").reshape(B * S, D).T),
        "wq_t": turned("L0_xattn_w_q"), "wk_t": turned("L0_xattn_w_k"),
        "wv_t": turned("L0_xattn_w_v"), "wo_t": turned("L0_xattn_w_o"),
        "w_ffn": np.ascontiguousarray(np.concatenate([fc, proj])),
        "lnw": np.ascontiguousarray(a("L0_ffn_ln_w").reshape(HB, P).T),
        "lnb": np.ascontiguousarray(a("L0_ffn_ln_b").reshape(HB, P).T),
        "gates": np.ascontiguousarray(np.broadcast_to(np.stack([a("g_xattn")[0], a("g_ffn")[0]]), (P, 2))),
    }
    nc = bacc.Bacc("TRN2", target_bir_lowering=False, num_devices=1)
    args = [nc.dram_tensor(n, v.shape, mybir.dt.from_np(v.dtype), kind="ExternalInput").ap() for n, v in arrays.items()]
    out = nc.dram_tensor("out", (B, T, D), mybir.dt.float32, kind="ExternalOutput").ap()
    build(nc, *args, out)
    r = run_bass_kernel_spmd(nc, [arrays], core_ids=[0])
    return r.results[0]["out"]
```
